# Optimizing a Trainium2 kernel written in Bass

```python
import numpy as np
import jax
import jax.numpy as jnp

def _softmax(x, axis=-1):
    return jax.nn.softmax(x, axis=axis)

def _gelu(x):
    return jax.nn.gelu(x, approximate=True)

def _silu(x):
    return jax.nn.silu(x)

def _sigmoid(x):
    return jax.nn.sigmoid(x)

def _layernorm(x, axis=-1, eps=1e-05):
    m = jnp.mean(x, axis=axis, keepdims=True)
    v = jnp.var(x, axis=axis, keepdims=True)
    return (x - m) / jnp.sqrt(v + eps)

def _scatter_add(tgt, idx, src, axis=0):
    return tgt.at[idx].add(src)

def _segment_sum(src, seg, n):
    return jax.ops.segment_sum(src, seg, n)
kernel_name = 'mk_recurrent_d1_jaxref_r4_f74a61'

def setup_inputs(seed: int=0):
    np.random.seed(seed)
    _w = jnp.asarray

    def _L0_attn_setup():
        import jax, jax.numpy as jnp
        import numpy as np
        B_, L_, D_ = (8, 512, 256)
        BD_ = 128
        DIN_ = 256
        NST_ = 16
        KC_ = 4
        DTR_ = 32

        def _silu(v):
            return v * jax.nn.sigmoid(v)

        def _forward(x, W_down, b_down, W_in, conv_w, conv_b, W_x, W_dt, b_dt, A_log, D_skip, W_out, ln_g, ln_b, W_up, b_up):
            h = x @ W_down + b_down
            xz = h @ W_in
            xc, z = jnp.split(xz, 2, axis=-1)
            L = xc.shape[1]
            xp = jnp.pad(xc, ((0, 0), (KC_ - 1, 0), (0, 0)))
            conv = conv_b + sum((xp[:, k:k + L, :] * conv_w[:, k] for k in range(KC_)))
            xc = _silu(conv)
            x_dbl = xc @ W_x
            dt_in = x_dbl[..., :DTR_]
            Bm = x_dbl[..., DTR_:DTR_ + NST_]
            Cm = x_dbl[..., DTR_ + NST_:]
            dt = jax.nn.softplus(dt_in @ W_dt + b_dt)
            A = -jnp.exp(A_log)

            def step(hprev, inp):
                dt_t, B_t, C_t, x_t = inp
                dA = jnp.exp(dt_t[:, :, None] * A)
                hnew = hprev * dA + (dt_t * x_t)[:, :, None] * B_t[:, None, :]
                y = jnp.einsum('bdn,bn->bd', hnew, C_t)
                return (hnew, y)
            h0 = jnp.zeros((xc.shape[0], DIN_, NST_), xc.dtype)
            seq = (dt.transpose(1, 0, 2), Bm.transpose(1, 0, 2), Cm.transpose(1, 0, 2), xc.transpose(1, 0, 2))
            _, ys = jax.lax.scan(step, h0, seq)
            y = ys.transpose(1, 0, 2) + D_skip * xc
            y = y * _silu(z)
            m = y @ W_out
            mu = m.mean(-1, keepdims=True)
            var = m.var(-1, keepdims=True)
            m = (m - mu) * jax.lax.rsqrt(var + 1e-05) * ln_g + ln_b
            return m @ W_up + b_up
        key = jax.random.key(seed)
        ks = jax.random.split(key, 10)
        s = 0.02
        x = jax.random.normal(ks[0], (B_, L_, D_), jnp.float32)
        W_down = jax.random.normal(ks[1], (D_, BD_), jnp.float32) * s
        b_down = jnp.zeros((BD_,), jnp.float32)
        W_in = jax.random.normal(ks[2], (BD_, 2 * DIN_), jnp.float32) * s
        conv_w = jax.random.normal(ks[3], (DIN_, KC_), jnp.float32) * 0.1
        conv_b = jnp.zeros((DIN_,), jnp.float32)
        W_x = jax.random.normal(ks[4], (DIN_, DTR_ + 2 * NST_), jnp.float32) * s
        W_dt = jax.random.normal(ks[5], (DTR_, DIN_), jnp.float32) * 0.1
        b_dt = jnp.full((DIN_,), -4.6, jnp.float32)
        A_log = jnp.log(jnp.broadcast_to(jnp.arange(1, NST_ + 1, dtype=jnp.float32), (DIN_, NST_)))
        D_skip = jnp.ones((DIN_,), jnp.float32)
        W_out = jax.random.normal(ks[6], (DIN_, BD_), jnp.float32) * s
        ln_g = jnp.ones((BD_,), jnp.float32)
        ln_b = jnp.zeros((BD_,), jnp.float32)
        W_up = jax.random.normal(ks[7], (BD_, D_), jnp.float32) * s
        b_up = jnp.zeros((D_,), jnp.float32)
        return dict(x=x, W_down=W_down, b_down=b_down, W_in=W_in, conv_w=conv_w, conv_b=conv_b, W_x=W_x, W_dt=W_dt, b_dt=b_dt, A_log=A_log, D_skip=D_skip, W_out=W_out, ln_g=ln_g, ln_b=ln_b, W_up=W_up, b_up=b_up)
    _L0_attn_in = _L0_attn_setup()

    def _L0_ffn_setup():
        import jax, jax.numpy as jnp
        import numpy as np
        B, T, D, H, E = (4, 512, 256, 512, 8)
        TOP_K = int(E * 0.25)
        key = jax.random.key(seed)
        ks = jax.random.split(key, 6)
        x = jax.random.normal(ks[0], (B, T, D), dtype=jnp.float32)
        gate = jax.random.normal(ks[1], (D, E), dtype=jnp.float32)
        W1 = jax.random.normal(ks[2], (E, D, H), dtype=jnp.float32) * D ** (-0.5)
        b1 = jnp.zeros((E, H), dtype=jnp.float32)
        W2 = jax.random.normal(ks[3], (E, H, D), dtype=jnp.float32) * H ** (-0.5)
        b2 = jnp.zeros((E, D), dtype=jnp.float32)
        return {'x': x, 'gate': gate, 'W1': W1, 'b1': b1, 'W2': W2, 'b2': b2}
    _L0_ffn_in = _L0_ffn_setup()
    _d = {'L0_attn_x': _L0_attn_in['x'], 'L0_attn_W_down': _L0_attn_in['W_down'], 'L0_attn_b_down': _L0_attn_in['b_down'], 'L0_attn_W_in': _L0_attn_in['W_in'], 'L0_attn_conv_w': _L0_attn_in['conv_w'], 'L0_attn_conv_b': _L0_attn_in['conv_b'], 'L0_attn_W_x': _L0_attn_in['W_x'], 'L0_attn_W_dt': _L0_attn_in['W_dt'], 'L0_attn_b_dt': _L0_attn_in['b_dt'], 'L0_attn_A_log': _L0_attn_in['A_log'], 'L0_attn_D_skip': _L0_attn_in['D_skip'], 'L0_attn_W_out': _L0_attn_in['W_out'], 'L0_attn_ln_g': _L0_attn_in['ln_g'], 'L0_attn_ln_b': _L0_attn_in['ln_b'], 'L0_attn_W_up': _L0_attn_in['W_up'], 'L0_attn_b_up': _L0_attn_in['b_up'], 'L0_ffn_gate': _L0_ffn_in['gate'], 'L0_ffn_W1': _L0_ffn_in['W1'], 'L0_ffn_b1': _L0_ffn_in['b1'], 'L0_ffn_W2': _L0_ffn_in['W2'], 'L0_ffn_b2': _L0_ffn_in['b2']}
    _x0 = _d['L0_attn_x']
    _d['L0_attn_x'] = jax.random.normal(jax.random.fold_in(jax.random.key(seed), 1), (16, 512, 256), dtype=_x0.dtype)
    del _x0
    return _d

def reference(L0_attn_x, L0_attn_W_down, L0_attn_b_down, L0_attn_W_in, L0_attn_conv_w, L0_attn_conv_b, L0_attn_W_x, L0_attn_W_dt, L0_attn_b_dt, L0_attn_A_log, L0_attn_D_skip, L0_attn_W_out, L0_attn_ln_g, L0_attn_ln_b, L0_attn_W_up, L0_attn_b_up, L0_ffn_gate, L0_ffn_W1, L0_ffn_b1, L0_ffn_W2, L0_ffn_b2):

    def _L0_attn_ref(x, W_down, b_down, W_in, conv_w, conv_b, W_x, W_dt, b_dt, A_log, D_skip, W_out, ln_g, ln_b, W_up, b_up):
        import jax, jax.numpy as jnp
        import numpy as np
        B_, L_, D_ = (8, 512, 256)
        BD_ = 128
        DIN_ = 256
        NST_ = 16
        KC_ = 4
        DTR_ = 32

        def _silu(v):
            return v * jax.nn.sigmoid(v)

        def _forward(x, W_down, b_down, W_in, conv_w, conv_b, W_x, W_dt, b_dt, A_log, D_skip, W_out, ln_g, ln_b, W_up, b_up):
            h = x @ W_down + b_down
            xz = h @ W_in
            xc, z = jnp.split(xz, 2, axis=-1)
            L = xc.shape[1]
            xp = jnp.pad(xc, ((0, 0), (KC_ - 1, 0), (0, 0)))
            conv = conv_b + sum((xp[:, k:k + L, :] * conv_w[:, k] for k in range(KC_)))
            xc = _silu(conv)
            x_dbl = xc @ W_x
            dt_in = x_dbl[..., :DTR_]
            Bm = x_dbl[..., DTR_:DTR_ + NST_]
            Cm = x_dbl[..., DTR_ + NST_:]
            dt = jax.nn.softplus(dt_in @ W_dt + b_dt)
            A = -jnp.exp(A_log)

            def step(hprev, inp):
                dt_t, B_t, C_t, x_t = inp
                dA = jnp.exp(dt_t[:, :, None] * A)
                hnew = hprev * dA + (dt_t * x_t)[:, :, None] * B_t[:, None, :]
                y = jnp.einsum('bdn,bn->bd', hnew, C_t)
                return (hnew, y)
            h0 = jnp.zeros((xc.shape[0], DIN_, NST_), xc.dtype)
            seq = (dt.transpose(1, 0, 2), Bm.transpose(1, 0, 2), Cm.transpose(1, 0, 2), xc.transpose(1, 0, 2))
            _, ys = jax.lax.scan(step, h0, seq)
            y = ys.transpose(1, 0, 2) + D_skip * xc
            y = y * _silu(z)
            m = y @ W_out
            mu = m.mean(-1, keepdims=True)
            var = m.var(-1, keepdims=True)
            m = (m - mu) * jax.lax.rsqrt(var + 1e-05) * ln_g + ln_b
            return m @ W_up + b_up
        return _forward(x, W_down, b_down, W_in, conv_w, conv_b, W_x, W_dt, b_dt, A_log, D_skip, W_out, ln_g, ln_b, W_up, b_up)

    def _L0_ffn_ref(x, gate, W1, b1, W2, b2):
        import jax, jax.numpy as jnp
        import numpy as np
        B, T, D, H, E = (4, 512, 256, 512, 8)
        TOP_K = int(E * 0.25)
        raw_gate = jax.nn.softmax(jnp.einsum('btd,de->bte', x, gate), axis=-1)
        topk_scores, topk_idx = jax.lax.top_k(raw_gate, TOP_K)
        mask = jax.nn.one_hot(topk_idx, E, dtype=raw_gate.dtype).sum(axis=-2)
        gate_topk = mask * raw_gate
        gate_topk = gate_topk / jnp.maximum(gate_topk.sum(axis=-1, keepdims=True), 1e-12)
        h = jax.nn.relu(jnp.einsum('btd,edh->beth', x, W1) + b1[None, :, None, :])
        expert_out = jnp.einsum('beth,ehd->betd', h, W2) + b2[None, :, None, :]
        out = jnp.einsum('bte,betd->btd', gate_topk, expert_out)
        return out
    x = L0_attn_x
    xn = _layernorm(x, axis=-1)
    s = _L0_attn_ref(xn, L0_attn_W_down, L0_attn_b_down, L0_attn_W_in, L0_attn_conv_w, L0_attn_conv_b, L0_attn_W_x, L0_attn_W_dt, L0_attn_b_dt, L0_attn_A_log, L0_attn_D_skip, L0_attn_W_out, L0_attn_ln_g, L0_attn_ln_b, L0_attn_W_up, L0_attn_b_up)
    g = _silu(_L0_ffn_ref(xn, L0_ffn_gate, L0_ffn_W1, L0_ffn_b1, L0_ffn_W2, L0_ffn_b2))
    x = x + s * g
    return x

_drawn_inputs = setup_inputs


def setup_inputs(seed=0):
    import zlib

    import numpy as np

    out = dict(_drawn_inputs(seed))
    spreads = {'L0_attn_b_down': (0.0, 0.8),
     'L0_attn_conv_b': (0.0, 0.42),
     'L0_attn_b_dt': (-4.599999904632568, 0.6),
     'L0_attn_D_skip': (1.0, 0.6),
     'L0_attn_ln_g': (1.0, 0.6),
     'L0_attn_ln_b': (0.0, 0.8),
     'L0_attn_b_up': (0.0, 0.1),
     'L0_ffn_b1': (0.0, 0.8),
     'L0_ffn_b2': (0.0, 0.8)}
    factors = {'L0_attn_W_down': 3.095,
     'L0_attn_W_in': 2.96,
     'L0_attn_conv_w': 8.0,
     'L0_attn_W_x': 8.0,
     'L0_attn_W_dt': 8.0,
     'L0_attn_A_log': 8.0,
     'L0_attn_W_out': 2.963}
    for name, (base, spread) in spreads.items():
        noise = np.random.default_rng([zlib.crc32(name.encode()), seed]).standard_normal(out[name].shape)
        drawn = base * np.exp(spread * noise) if base else spread * noise
        out[name] = jnp.asarray(drawn.astype(out[name].dtype))
    for name, factor in factors.items():
        out[name] = (out[name] * factor).astype(out[name].dtype)
    return out
```

```python
from contextlib import ExitStack

import concourse.bass as bass
from concourse import mybir

ALU = mybir.AluOpType
ACT = mybir.ActivationFunctionType
AX = mybir.AxisListType
F32 = mybir.dt.float32
BF16 = mybir.dt.bfloat16

P = 128
NSEQ, L, D = 16, 512, 256
TT = L // P
KD = D // P
BD = 128
DIN = 256
NH = DIN // P
NST = 16
TAPS = 4
DTR = 32
E, HID = 8, 512
KH = HID // P
TOP_K = 2
EPS = 1e-5
LAG = 2

FRONT = ["T0", "T1", "G", "H", "V0", "V1", "Z0", "Z1", "GT", "X", "D0", "D1"]
FRONT_AT = {1: ["T0", "T1"], 2: ["G", "H"], 4: ["V0", "V1"], 5: ["Z0", "Z1"], 8: ["GT", "X"], 9: ["D0", "D1"]}
BACK = ["M", "MT", "S0", "S1"]
BACK_AT = {3: ["M"], 5: ["MT"], 6: ["S0", "S1"]}


def expert_jobs():
    steps = []
    for e in range(E):
        steps.append(([("gb", 0, 0), ("gb", 0, 1)] if e == 0 else []) + [("h", e, 0), ("h", e, 1)]
                     + ([("o", e - 1, 0)] if e else []))
        steps.append([("h", e, 2), ("h", e, 3)] + ([("o", e - 1, 1)] if e else []))
    steps[-1] += [("o", E - 1, 0), ("o", E - 1, 1)]
    return steps


EXPERT_STEPS = expert_jobs()
EXPERT_POS = {job: i for i, job in enumerate(j for step in EXPERT_STEPS for j in step)}
NFF = len(EXPERT_POS)
ACC_STEPS = 2 + E * TT


def build(nc, x, W_down, b_down, W_in, conv_w, conv_b, W_x, W_dt, b_dt, A_log, D_skip, W_out, ln_g, ln_b,
          W_up, b_up, gate, W1, b1, W2, b2, out):
    with ExitStack() as ctx:
        def sb(name, shape, dt=F32):
            return ctx.enter_context(nc.sbuf_tensor(name, shape, dt))

        def ps(name):
            return ctx.enter_context(nc.psum_tensor(name, [P, 512], F32))

        def sem(name):
            return ctx.enter_context(nc.semaphore(name))

        w_down = sb("w_down", [P, KD, BD])
        w_in = sb("w_in", [P, 2 * DIN])
        w_conv = sb("w_conv", [P, TAPS, DIN])
        w_x = sb("w_x", [P, NH, 2 * NST + DTR])
        w_dt = sb("w_dt", [64, DIN])
        w_out = sb("w_out", [P, NH, BD])
        w_up = sb("w_up", [P, D])
        w_up_g = sb("w_up_g", [P, D])
        w_gate = sb("w_gate", [P, KD, E])
        w1 = sb("w1", [P, E, KD, HID])
        w2 = sb("w2", [P, E, KH, D])
        b1_c = sb("b1_c", [P, E, KH])
        b2_r = sb("b2_r", [E, D])
        b_down_c = sb("b_down_c", [P, 1])
        conv_w_c = sb("conv_w_c", [P, NH, TAPS])
        conv_b_c = sb("conv_b_c", [P, NH])
        b_dt_c = sb("b_dt_c", [P, NH])
        a_log_c = sb("a_log_c", [P, NH, NST])
        a_exp = sb("a_exp", [P, NH, NST])
        a_neg = sb("a_neg", [P, NH, NST])
        d_skip_c = sb("d_skip_c", [P, NH])
        ln_g_c = sb("ln_g_c", [P, 1])
        ln_b_c = sb("ln_b_c", [P, 1])
        ln_b_wide = sb("ln_b_wide", [P, P])
        b_up_r = sb("b_up_r", [P, D])
        up_const = sb("up_const", [P, D])
        ident = sb("ident", [P, P])
        ones = sb("ones", [P, P])
        select = sb("select", [96, 2 * NST, P], BF16)
        lower = sb("lower", [P, E, E])
        eps_c = sb("eps_c", [P, 1])

        x_in = sb("x_in", [P, TT, D])
        ln_stats = sb("ln_stats", [P, TT, 6])
        ln_mv = sb("ln_mv", [P, TT, 2])
        ln_log = sb("ln_log", [P, TT])
        ln_rstd = sb("ln_rstd", [P, TT])
        xnT = sb("xnT", [P, 2, KD, L])
        logits = sb("logits", [P, TT, E])
        lmax = sb("lmax", [P, TT])
        lexp = sb("lexp", [P, TT, E])
        lsum = sb("lsum", [P, TT])
        linv = sb("linv", [P, TT])
        prob = sb("prob", [P, TT, E])
        above = sb("above", [P, TT, E, E])
        equal = sb("equal", [P, TT, E, E])
        rank = sb("rank", [P, TT, E])
        mask = sb("mask", [P, TT, E])
        picked = sb("picked", [P, TT, E])
        psum_k = sb("psum_k", [P, TT])
        pguard = sb("pguard", [P, TT])
        pinv = sb("pinv", [P, TT])
        gates = sb("gates", [P, 2, TT, E])
        gatesT = sb("gatesT", [E, L])
        h_pad = sb("h_pad", [P, TAPS - 1 + L])
        xz = sb("xz", [P, 2, 2 * NH, L])
        xdbl = sb("xdbl", [64, L])
        bc = sb("bc", [96, 2, L], BF16)
        bc_rest = sb("bc_rest", [32, L])
        bc_mid = sb("bc_mid", [32, L], BF16)
        dt_v = sb("dt_v", [P, NH, L])
        dt_m = sb("dt_m", [P, NH, L])
        dt = sb("dt", [P, 2, NH, L])
        u = sb("u", [P, 2, NH, L])

        decay = sb("decay", [P, 2, NH, L])
        drive = sb("drive", [P, NH, L])
        state = sb("state", [P, 2, NH, L])
        c_wide = sb("c_wide", [P, 2, L])

        skip = dt_m
        mix = dt_v[:, :, :].rearrange("p h (c d) -> p (h c) d", d=D)
        hT = sb("hT", [P, 2, KH, L])
        acc = sb("acc", [P, 2, TT, D])
        tap_diag = hT[:, 0, 0:2, :].rearrange("p a (b m) -> p (a b) m", b=4).rearrange("p (t h) m -> p t h m", h=NH)

        m_sb = dt_m[:, 0, :].rearrange("p (c m) -> p c m", c=TT)
        m_stats = sb("m_stats", [P, TT, 6])
        m_mv = sb("m_mv", [P, TT, 2])
        m_log = sb("m_log", [P, TT])
        m_rstd = sb("m_rstd", [P, TT])
        mnT = dt_m[:, 1, :]
        res = sb("res", [P, TT, D])

        pB = [ps("pB0"), ps("pB1")]
        pC = ps("pC")
        pY = [ps("pY0"), ps("pY1")]
        pF = [ps("pF0"), ps("pF1")]
        pM = ps("pM")

        w_ready = sem("w_ready")
        w_ffn_ready = sem("w_ffn_ready")
        x_loaded = sem("x_loaded")
        xres_loaded = sem("xres_loaded")
        stored = sem("stored")
        consts_base = sem("consts_base")
        consts_ready = sem("consts_ready")
        taps_diag = sem("taps_diag")
        taps_wide = sem("taps_wide")
        w_made = sem("w_made")
        lnb_wide = sem("lnb_wide")
        lnb_up = sem("lnb_up")
        a_exp_ready = sem("a_exp_ready")
        a_ready = sem("a_ready")
        stats_step = sem("stats_step")
        rstd_step = sem("rstd_step")
        xn_ready = sem("xn_ready")
        front_filled = sem("front_filled")
        front_drained = sem("front_drained")
        back_filled = sem("back_filled")
        back_drained = sem("back_drained")
        gate_step = sem("gate_step")
        gate_exp = sem("gate_exp")
        gates_ready = sem("gates_ready")
        pick_step = sem("pick_step")
        dve_passed = sem("dve_passed")
        pool_passed = sem("pool_passed")
        consts_pool = sem("consts_pool")
        silu_done = sem("silu_done")
        split_step = sem("split_step")
        bc_shifted = sem("bc_shifted")
        negabs_ready = sem("negabs_ready")
        dt_exp = sem("dt_exp")
        dt_ln = sem("dt_ln")
        onep_ready = sem("onep_ready")
        dt_rest = sem("dt_rest")
        dt_ready = sem("dt_ready")
        u_ready = sem("u_ready")
        b_wide_ready = sem("b_wide_ready")
        c_wide_ready = sem("c_wide_ready")
        c_copied = sem("c_copied")
        decay_ready = sem("decay_ready")
        drive_ready = sem("drive_ready")
        scanned = sem("scanned")
        seen_ready = sem("seen_ready")
        summed = sem("summed")
        y_read = sem("y_read")
        gated = sem("gated")
        m_stats_step = sem("m_stats_step")
        m_rstd_step = sem("m_rstd_step")
        mn_ready = sem("mn_ready")
        ffn_gate_ready = sem("ffn_gate_ready")
        mixed = sem("mixed")
        out_ready = sem("out_ready")
        ffn_filled = sem("ffn_filled")
        ffn_free = [sem("ffn_free0"), sem("ffn_free1")]
        relu_done = sem("relu_done")
        acc_step = sem("acc_step")

        def front_count(f, job):
            return f * len(FRONT) + FRONT.index(job) + 1

        def back_count(b, job):
            return b * len(BACK) + BACK.index(job) + 1

        x_v = x.rearrange("s (c p) d -> s p c d", p=P)
        out_v = out.rearrange("s (c p) d -> s p c d", p=P)

        def column(v, n):
            return v.rearrange("(c p) -> p c", p=P) if n > 1 else v.rearrange("(p c) -> p c", c=1)

        small_loads = [
            (w_down[:, :, :], W_down.rearrange("(k p) m -> p k m", p=P)),
            (w_in[:, :], W_in),
            (w_x[:, :, 0:2 * NST], W_x.rearrange("(k p) m -> p k m", p=P)[:, :, DTR:]),
            (w_x[:, :, 2 * NST:], W_x.rearrange("(k p) m -> p k m", p=P)[:, :, 0:DTR]),
            (w_dt[32:64, :], W_dt),
            (w_out[:, :, :], W_out.rearrange("(k p) m -> p k m", p=P)),
            (w_up[:, :], W_up),
            (w_gate[:, :, :], gate.rearrange("(k p) m -> p k m", p=P)),
            (b_down_c[:, :], column(b_down, 1)),
            (conv_w_c[:, :, :], conv_w.rearrange("(c p) k -> p c k", p=P)),
            (conv_b_c[:, :], column(conv_b, NH)),
            (b_dt_c[:, :], column(b_dt, NH)),
            (a_log_c[:, :, :], A_log.rearrange("(c p) n -> p c n", p=P)),
            (d_skip_c[:, :], column(D_skip, NH)),
            (ln_g_c[:, :], column(ln_g, 1)),
            (ln_b_c[:, :], column(ln_b, 1)),
            (b_up_r[:, :], b_up.partition_broadcast(P)),
        ]
        n_small = 16 * len(small_loads)

        block = ctx.enter_context(nc.Block())

        @block.sync
        def _(sp):
            def load_x(f):
                sp.wait_ge(front_filled, front_count(f - 1, "T1"))
                sp.dma_start(x_in[:, :, :], x_v[f]).then_inc(x_loaded, 16)

            def load_residual(b):
                sp.wait_ge(stored, 16 * b)
                sp.dma_start(res[:, :, :], x_v[b]).then_inc(xres_loaded, 16)

            def store(b):
                sp.wait_ge(out_ready, b + 1)
                sp.dma_start(out_v[b], res[:, :, :]).then_inc(stored, 16)

            sp.dma_start(x_in[:, :, :], x_v[0]).then_inc(x_loaded, 16)
            for dst, src in small_loads:
                with nc.allow_non_contiguous_dma(reason="bias columns, once"):
                    sp.dma_start(dst, src).then_inc(w_ready, 16)
            with nc.allow_non_contiguous_dma(reason="bias columns, once"):
                sp.dma_start(b1_c[:, :, :], b1.rearrange("e (c p) -> p e c", p=P)).then_inc(w_ffn_ready, 16)
            sp.dma_start(b2_r[:, :], b2).then_inc(w_ffn_ready, 16)
            for e in range(E):
                sp.dma_start(w1[:, e, :, :], W1[e].rearrange("(k p) h -> p k h", p=P)).then_inc(w_ffn_ready, 16)
                sp.dma_start(w2[:, e, :, :], W2[e].rearrange("(k p) d -> p k d", p=P)).then_inc(w_ffn_ready, 16)
            load_x(1)

            load_residual(0)
            load_x(2)
            store(0)
            with sp.Fori(1, NSEQ - 2) as s:
                load_residual(s)
                load_x(s + 2)
                store(s)
            for b in (NSEQ - 2, NSEQ - 1):
                load_residual(b)
                store(b)
            sp.wait_ge(stored, 16 * NSEQ)

        n_ffn = 16 * (2 + 2 * E)

        @block.tensor
        def _(pe):
            mm = nc.tensor.matmul

            def spread(s, q, n):
                g = s * NST + n
                if n == 0:
                    pe.wait_ge(split_step, 4 * (s + 1))
                    pe.wait_ge(bc_shifted, 2 * (s + 1))
                if n >= 2 or not isinstance(s, int) or s > 0:
                    pe.wait_ge(drive_ready, g - 1)
                mm(pB[n % 2][:, :], select[:, n, :], bc[:, q, :], start=True, stop=True).then_inc(b_wide_ready, 1)
                pe.wait_ge(c_copied, g)
                mm(pC[:, :], select[:, NST + n, :], bc[:, q, :], start=True, stop=True).then_inc(c_wide_ready, 1)

            def add_up(s, n):
                pe.wait_ge(seen_ready, s * NST + n + 1)
                if n == 0:
                    pe.wait_ge(y_read, s)
                for half in range(NH):
                    last = mm(pY[half][:, :], ident[:, :], state[:, n % 2, half, :],
                              start=(n == 0), stop=(n == NST - 1), skip_group_check=True)
                last.then_inc(summed, 1)

            def bank_free(front_done, back_done):
                if front_done is not None:
                    pe.wait_ge(front_drained, front_done)
                if back_done is not None:
                    pe.wait_ge(back_drained, back_done)

            def front_job(f, q, job, back_done):
                bank_free(front_count(f, job) - 1, back_done)
                if job in ("T0", "T1"):
                    pe.wait_ge(xn_ready, f + 1)
                    k = int(job[1])
                    for c in range(TT):
                        last = nc.tensor.transpose(pM[:, c * P:(c + 1) * P], x_in[:, c, k * P:(k + 1) * P], ident[:, :])
                elif job == "G":
                    for c in range(TT):
                        for k in range(KD):
                            last = mm(pM[:, c * E:(c + 1) * E], xnT[:, q, k, c * P:(c + 1) * P], w_gate[:, k, :],
                                      start=(k == 0), stop=(k == KD - 1))
                elif job == "H":
                    for k in range(KD):
                        last = mm(pM[:, :], w_down[:, k, :], xnT[:, q, k, :], start=(k == 0), stop=(k == KD - 1))
                elif job in ("V0", "V1"):
                    half = int(job[1])
                    for t in range(TAPS):
                        last = mm(pM[:, :], w_conv[:, t, half * P:(half + 1) * P], h_pad[:, t:t + L],
                                  start=(t == 0), stop=(t == TAPS - 1))
                elif job in ("Z0", "Z1"):
                    half = int(job[1])
                    last = mm(pM[:, :], w_in[:, DIN + half * P:DIN + (half + 1) * P], h_pad[:, TAPS - 1:],
                              start=True, stop=True)
                elif job == "GT":
                    pe.wait_ge(gates_ready, f + 1)
                    for c in range(TT):
                        last = nc.tensor.transpose(pM[0:E, c * P:(c + 1) * P], gates[:, q, c, :], ident[:, :])
                elif job == "X":
                    pe.wait_ge(silu_done, f + 1)
                    for k in range(NH):
                        last = mm(pM[0:64, :], w_x[:, k, :], xz[:, q, k, :], start=(k == 0), stop=(k == NH - 1))
                else:
                    half = int(job[1])
                    last = mm(pM[:, :], w_dt[32:64, half * P:(half + 1) * P], xdbl[32:64, :], start=True, stop=True)
                last.then_inc(front_filled, 1)

            def back_job(b, job, front_done):
                bank_free(front_done, None if job == BACK[0] else back_count(b, job) - 1)
                if job == "M":
                    pe.wait_ge(gated, b + 1)
                    for c in range(TT):
                        for k in range(NH):
                            last = mm(pM[:, c * BD:(c + 1) * BD], skip[:, k, c * P:(c + 1) * P], w_out[:, k, :],
                                      start=(k == 0), stop=(k == NH - 1))
                elif job == "MT":
                    pe.wait_ge(mn_ready, b + 1)
                    for c in range(TT):
                        last = nc.tensor.transpose(pM[:, c * P:(c + 1) * P], m_sb[:, c, :], ident[:, :])
                else:
                    j = int(job[1])
                    for c in range(2):
                        t = 2 * j + c
                        last = mm(pM[:, c * D:(c + 1) * D], mnT[:, t * P:(t + 1) * P], w_up_g[:, :],
                                  start=True, stop=True)
                last.then_inc(back_filled, 1)

            def expert_job(s, q, job):
                kind, e, i = job
                pos = EXPERT_POS[job]
                bank = pF[pos % 2]
                if pos >= 2 or not isinstance(s, int) or s > 0:
                    pe.wait_ge(ffn_free[pos % 2], s * (NFF // 2) + pos // 2)
                if kind == "gb":
                    for c in range(2):
                        t = 2 * i + c
                        last = mm(bank[:, c * D:(c + 1) * D], gatesT[:, t * P:(t + 1) * P], b2_r[:, :],
                                  start=True, stop=True)
                elif kind == "h":
                    for k in range(KD):
                        last = mm(bank[:, :], w1[:, e, k, i * P:(i + 1) * P], xnT[:, q, k, :],
                                  start=(k == 0), stop=(k == KD - 1))
                else:
                    pe.wait_ge(relu_done, s * E * KH + (e + 1) * KH)
                    for c in range(2):
                        t = 2 * i + c
                        for k in range(KH):
                            last = mm(bank[:, c * D:(c + 1) * D], hT[:, e % 2, k, t * P:(t + 1) * P], w2[:, e, k, :],
                                      start=(k == 0), stop=(k == KH - 1))
                last.then_inc(ffn_filled, 1)

            def sequence(s, q, first=False, last=False):
                f_done, b_done = (s + 1) * len(FRONT), None
                for n in range(NST):
                    spread(s, q, n)
                    if n >= LAG:
                        add_up(s, n - LAG)
                    elif not first:
                        add_up(s - 1, NST - LAG + n)
                    for job in EXPERT_STEPS[n]:
                        expert_job(s, q, job)
                    for job in [] if last else FRONT_AT.get(n, []):
                        front_job(s + 1, 1 - q, job, b_done)
                        f_done = f_done + 1
                    for job in [] if first else BACK_AT.get(n, []):
                        back_job(s - 1, job, f_done)
                        b_done = back_count(s - 1, job)

            pe.wait_ge(consts_base, 3)
            pe.wait_ge(taps_diag, TAPS * NH)
            for t in range(TAPS):
                for half in range(NH):
                    at = (t % 2) * DIN + half * P
                    last = mm(pF[t // 2][:, at:at + P], ones[:, :], tap_diag[:, t, half, :], start=True, stop=True)
                last.then_inc(taps_wide, 1)
            pe.wait_ge(lnb_wide, 1)
            pe.wait_ge(w_ready, n_small)
            mm(pM[:, 0:D], ln_b_wide[:, :], w_up[:, :], start=True, stop=True).then_inc(lnb_up, 1)
            pe.wait_ge(w_made, TAPS + 3)
            pe.wait_ge(consts_ready, 7)

            for job in FRONT:
                front_job(0, 0, job, None)
            pe.wait_ge(w_ffn_ready, n_ffn)
            sequence(0, 0, first=True)
            with pe.Fori(1, NSEQ - 1, 2) as s:
                sequence(s, 1)
                sequence(s + 1, 0)
            sequence(NSEQ - 1, 1, last=True)
            for n in range(NST - LAG, NST):
                add_up(NSEQ - 1, n)
            for job in BACK:
                back_job(NSEQ - 1, job, NSEQ * len(FRONT))

        @block.scalar
        def _(act):
            act_fn = nc.scalar.activation

            def c_copy(s, n):
                g = s * NST + n
                act.wait_ge(c_wide_ready, g + 1)
                if n >= 2 or not isinstance(s, int) or s > 0:
                    act.wait_ge(seen_ready, g - 1)
                nc.scalar.copy(c_wide[:, n % 2, :], pC[:, :]).then_inc(c_copied, 1)

            def decays(s, q, n):
                g = s * NST + n
                if n == 0:
                    act.wait_ge(dt_ready, s + 1)
                if n >= 2 or not isinstance(s, int) or s > 0:
                    act.wait_ge(scanned, g - 1)
                for half in range(NH):
                    last = act_fn(decay[:, n % 2, half, 1:], dt[:, q, half, 1:], ACT.Exp,
                                  scale=a_neg[:, half, n:n + 1])
                last.then_inc(decay_ready, 1)

            def hidden(s, job):
                kind, e, i = job
                if kind != "h":
                    return
                pos = EXPERT_POS[job]
                act.wait_ge(ffn_filled, s * NFF + pos + 1)
                act_fn(hT[:, e % 2, i, :], pF[pos % 2][:, :], ACT.Relu, bias=b1_c[:, e, i:i + 1]).then_inc(
                    ffn_free[pos % 2], 1)
                act.wait_ge(ffn_free[pos % 2], s * (NFF // 2) + pos // 2 + 1)
                act.sem_inc(relu_done, 1)

            def rstd(count, step, stats, mv, log, dst):
                act.wait_ge(stats, 2 * count)
                act_fn(log[:, :], mv[:, :, 1], ACT.Ln, bias=eps_c[:, :]).then_inc(step, 1)
                act.wait_ge(step, 2 * count - 1)
                act_fn(dst[:, :], log[:, :], ACT.Exp, scale=-0.5).then_inc(step, 1)

            def front_drain(f, q, job):
                act.wait_ge(front_filled, front_count(f, job))
                i = int(job[1]) if job[1:].isdigit() else 0
                if job[0] == "T":
                    ins = nc.scalar.copy(xnT[:, q, i, :], pM[:, :])
                elif job == "H":
                    ins = act_fn(h_pad[:, TAPS - 1:], pM[:, :], ACT.Identity, bias=b_down_c[:, :])
                elif job[0] == "V":
                    if job == "V0" and (not isinstance(f, int) or f > 1):
                        act.wait_ge(gated, f - 1)
                    ins = act_fn(xz[:, q, i, :], pM[:, :], ACT.Identity, bias=conv_b_c[:, i:i + 1])
                elif job[0] == "Z":
                    ins = nc.scalar.copy(xz[:, q, NH + i, :], pM[:, :])
                elif job == "GT":
                    ins = nc.scalar.copy(gatesT[:, :], pM[0:E, :])
                elif job == "X":
                    ins = nc.scalar.copy(xdbl[:, :], pM[0:64, :])
                else:
                    if not isinstance(f, int) or f > 1:
                        act.wait_ge(out_ready, f - 1)
                    ins = act_fn(dt_v[:, i, :], pM[:, :], ACT.Identity, bias=b_dt_c[:, i:i + 1])
                ins.then_inc(front_drained, 1)

            def silu_front(f, q):
                act.wait_ge(front_drained, front_count(f, "Z1"))
                act_fn(xz[:, q, :, :], xz[:, q, :, :], ACT.Silu).then_inc(silu_done, 1)

            def silu_experts(b, qb):
                act.wait_ge(acc_step, (b + 1) * ACC_STEPS)
                act_fn(acc[:, qb, :, :], acc[:, qb, :, :], ACT.Silu).then_inc(ffn_gate_ready, 1)

            def gate_exps(f):
                act.wait_ge(gate_step, 9 * f + 3)
                act_fn(lexp[:, :, :], lexp[:, :, :], ACT.Exp).then_inc(gate_exp, 1)

            def shift_parts(f, q):
                act.wait_ge(split_step, 4 * (f + 1))
                nc.scalar.copy(bc[32:64, q, :], bc_mid[:, :]).then_inc(bc_shifted, 1)
                nc.scalar.copy(bc[64:96, q, :], bc_rest[:, :]).then_inc(bc_shifted, 1)

            def dt_exps(f, q):
                act.wait_ge(negabs_ready, f + 1)
                act_fn(u[:, q, :, :], dt_m[:, :, :], ACT.Exp).then_inc(dt_exp, 1)
                act.wait_ge(dt_exp, f + 1)
                act_fn(dt[:, q, :, :], u[:, q, :, :], ACT.Ln, bias=1.0).then_inc(dt_ln, 1)

            def back_copy(b, job):
                act.wait_ge(back_filled, back_count(b, job))
                dst = m_sb[:, :, :] if job == "M" else mnT[:, :]
                src = pM[:, :].rearrange("p (c m) -> p c m", c=TT) if job == "M" else pM[:, :]
                nc.scalar.copy(dst, src).then_inc(back_drained, 1)

            def front_step(f, q, n):
                if n == 0:
                    rstd(f + 1, rstd_step, stats_step, ln_mv, ln_log, ln_rstd)
                if n == 3:
                    gate_exps(f)
                for job in FRONT_AT.get(n, []):
                    if job != "G":
                        front_drain(f, q, job)
                if n == 6:
                    silu_front(f, q)
                if n == 9:
                    shift_parts(f, q)
                if n == 11:
                    dt_exps(f, q)

            def back_step(b, qb, n):
                if n == 3:
                    back_copy(b, "M")
                if n == 4:
                    rstd(b + 1, m_rstd_step, m_stats_step, m_mv, m_log, m_rstd)
                if n == 5:
                    back_copy(b, "MT")
                if n == 6:
                    silu_experts(b, qb)

            def sequence(s, q, first=False, last=False):
                for n in range(NST):
                    c_copy(s, n)
                    decays(s, q, n)
                    for job in EXPERT_STEPS[n]:
                        hidden(s, job)
                    if not last:
                        front_step(s + 1, 1 - q, n)
                    if not first:
                        back_step(s - 1, 1 - q, n)

            act.wait_ge(w_ready, n_small)
            act_fn(a_exp[:, :, :], a_log_c[:, :, :], ACT.Exp).then_inc(a_exp_ready, 1)
            act.wait_ge(a_exp_ready, 1)
            nc.scalar.mul(a_neg[:, :, :], a_exp[:, :, :], -1.0).then_inc(a_ready, 1)
            act.wait_ge(a_ready, 1)
            act.wait_ge(consts_ready, 7)
            for n in range(NST):
                front_step(0, 0, n)
            act.wait_ge(w_ffn_ready, n_ffn)
            sequence(0, 0, first=True)
            with act.Fori(1, NSEQ - 1, 2) as s:
                sequence(s, 1)
                sequence(s + 1, 0)
            sequence(NSEQ - 1, 1, last=True)
            for n in range(NST):
                back_step(NSEQ - 1, 1, n)

        @block.vector
        def _(dve):
            tt, ts, stt = nc.vector.tensor_tensor, nc.vector.tensor_scalar, nc.vector.scalar_tensor_tensor

            def scan(s, q, n):
                g = s * NST + n
                dve.wait_ge(b_wide_ready, g + 1)
                if n == 0:
                    dve.wait_ge(u_ready, s + 1)
                dve.wait_ge(scanned, g)
                tt(drive[:, :, :], u[:, q, :, :],
                   pB[n % 2][:, :].unsqueeze(1).broadcast_to([P, NH, L]), ALU.mult).then_inc(drive_ready, 1)
                dve.wait_ge(drive_ready, g + 1)
                dve.wait_ge(decay_ready, g + 1)
                if n >= 2 or not isinstance(s, int) or s > 0:
                    dve.wait_ge(summed, g - 1)
                flat = "p h t -> p (h t)"
                nc.vector.tensor_tensor_scan(state[:, n % 2, :, :].rearrange(flat),
                                             decay[:, n % 2, :, :].rearrange(flat),
                                             drive[:, :, :].rearrange(flat),
                                             0.0, ALU.mult, ALU.add).then_inc(scanned, 1)

            def add_expert(s, q, job):
                kind, e, i = job
                if kind == "h":
                    return
                pos = EXPERT_POS[job]
                dve.wait_ge(ffn_filled, s * NFF + pos + 1)
                bank = pF[pos % 2][:, :].rearrange("p (c d) -> p c d", c=2)
                base = s * ACC_STEPS
                if kind == "gb":
                    nc.vector.tensor_copy(acc[:, q, 2 * i:2 * i + 2, :], bank).then_inc(acc_step, 1)
                    dve.wait_ge(acc_step, base + i + 1)
                    dve.sem_inc(ffn_free[pos % 2], 1)
                    return
                for c in range(2):
                    t = 2 * i + c
                    dve.wait_ge(acc_step, base + (2 if e == 0 else 2 + (e - 1) * TT + t + 1))
                    stt(acc[:, q, t, :], bank[:, c, :], gates[:, q, t, e:e + 1], acc[:, q, t, :],
                        ALU.mult, ALU.add).then_inc(acc_step, 1)
                dve.wait_ge(acc_step, base + 2 + e * TT + 2 * i + 2)
                dve.sem_inc(ffn_free[pos % 2], 1)

            def statistics(count, step, src, stats, mv):
                for c in range(TT):
                    last = nc.vector.bn_stats(stats[:, c, :], src[:, c, :])
                last.then_inc(step, 1)
                dve.wait_ge(step, 2 * count - 1)
                dve.sem_inc(dve_passed, 1)
                for c in range(TT):
                    last = nc.vector.bn_aggr(mv[:, c, :], stats[:, c, :])
                last.then_inc(step, 1)
                dve.wait_ge(step, 2 * count)

            def normalise(f):
                dve.wait_ge(rstd_step, 2 * (f + 1))
                for c in range(TT):
                    last = ts(x_in[:, c, :], x_in[:, c, :], ln_mv[:, c, 0:1], ln_rstd[:, c:c + 1],
                              ALU.subtract, ALU.mult)
                last.then_inc(xn_ready, 1)

            def wide(v):
                return v[:, :].unsqueeze(2).broadcast_to([P, TT, E])

            def read_logits(f):
                dve.wait_ge(front_filled, front_count(f, "G"))
                nc.vector.tensor_copy(logits[:, :, :], pM[:, 0:TT * E].rearrange("p (c e) -> p c e", c=TT)).then_inc(
                    front_drained, 1)
                dve.wait_ge(front_drained, front_count(f, "G"))
                dve.sem_inc(gate_step, 1)

            def route(f, q):
                count = 9 * f + 1

                def step(ins):
                    nonlocal count
                    ins.then_inc(gate_step, 1)
                    count = count + 1
                    dve.wait_ge(gate_step, count)

                step(nc.vector.tensor_reduce(lmax[:, :], logits[:, :, :], AX.X, ALU.max))
                step(tt(lexp[:, :, :], logits[:, :, :], wide(lmax), ALU.subtract))
                dve.wait_ge(gate_exp, f + 1)
                step(nc.vector.tensor_reduce(lsum[:, :], lexp[:, :, :], AX.X, ALU.add))
                step(nc.vector.reciprocal(linv[:, :], lsum[:, :]))
                step(tt(prob[:, :, :], lexp[:, :, :], wide(linv), ALU.mult))
                rows = prob[:, :, :].unsqueeze(2).broadcast_to([P, TT, E, E])
                cols = prob[:, :, :].unsqueeze(3).broadcast_to([P, TT, E, E])
                tt(above[:, :, :, :], rows, cols, ALU.is_gt)
                step(tt(equal[:, :, :, :], rows, cols, ALU.is_equal))
                low = lower[:, :, :].rearrange("p i j -> p (i j)").unsqueeze(1).broadcast_to([P, TT, E * E])
                flat = "p c i j -> p c (i j)"
                step(tt(equal[:, :, :, :].rearrange(flat), equal[:, :, :, :].rearrange(flat), low, ALU.mult))
                step(tt(above[:, :, :, :], above[:, :, :, :], equal[:, :, :, :], ALU.add))
                return count

            def pick(f, q):
                nc.vector.tensor_reduce(rank[:, :, :], above[:, :, :, :], AX.X, ALU.add).then_inc(pick_step, 1)
                dve.wait_ge(pick_step, 6 * f + 1)
                ts(mask[:, :, :], rank[:, :, :], float(TOP_K), None, ALU.is_lt).then_inc(pick_step, 1)
                dve.wait_ge(pick_step, 6 * f + 2)
                tt(picked[:, :, :], mask[:, :, :], prob[:, :, :], ALU.mult).then_inc(pick_step, 1)
                dve.wait_ge(pick_step, 6 * f + 3)
                nc.vector.tensor_reduce(psum_k[:, :], picked[:, :, :], AX.X, ALU.add).then_inc(pick_step, 1)
                dve.wait_ge(pick_step, 6 * f + 4)
                ts(pguard[:, :], psum_k[:, :], 1e-12, None, ALU.max).then_inc(pick_step, 1)
                dve.wait_ge(pick_step, 6 * f + 5)
                nc.vector.reciprocal(pinv[:, :], pguard[:, :]).then_inc(pick_step, 1)
                dve.wait_ge(pick_step, 6 * f + 6)
                tt(gates[:, q, :, :], picked[:, :, :], wide(pinv), ALU.mult).then_inc(gates_ready, 1)

            def front_step(f, q, n):
                if n == 0:
                    dve.wait_ge(x_loaded, 16 * (f + 1))
                    statistics(f + 1, stats_step, x_in, ln_stats, ln_mv)
                    normalise(f)
                if n == 2:
                    read_logits(f)
                if n == 3:
                    route(f, q)
                    pick(f, q)
                if n == 10:
                    dve.wait_ge(front_drained, front_count(f, "D1"))
                    if not isinstance(f, int) or f > 0:
                        dve.wait_ge(u_ready, f)
                    stt(dt_m[:, :, :], dt_v[:, :, :], -1.0, dt_v[:, :, :], ALU.mult, ALU.min).then_inc(
                        negabs_ready, 1)
                if n == 12:
                    dve.wait_ge(dt_exp, f + 1)
                    ts(dt_m[:, :, :], u[:, q, :, :], 1.0, 1.0, ALU.add, ALU.subtract).then_inc(onep_ready, 1)
                if n == 13:
                    dve.wait_ge(dt_rest, 2 * (f + 1))
                    stt(dt[:, q, :, :], dt_v[:, :, :], 0.0, dt_m[:, :, :], ALU.max, ALU.add).then_inc(dt_ready, 1)

            def back_step(b, qb, n):
                if n == 2:
                    dve.wait_ge(summed, NST * (b + 1))
                    for half in range(NH):
                        last = stt(skip[:, half, :], xz[:, qb, half, :], d_skip_c[:, half:half + 1],
                                   pY[half][:, :], ALU.mult, ALU.add)
                    last.then_inc(y_read, 1)
                if n == 4:
                    dve.wait_ge(back_drained, back_count(b, "M"))
                    statistics(b + 1, m_stats_step, m_sb, m_stats, m_mv)
                    dve.wait_ge(m_rstd_step, 2 * (b + 1))
                    for c in range(TT):
                        last = ts(m_sb[:, c, :], m_sb[:, c, :], m_mv[:, c, 0:1], m_rstd[:, c:c + 1],
                                  ALU.subtract, ALU.mult)
                    last.then_inc(mn_ready, 1)
                if n == 6:
                    for j in range(2):
                        dve.wait_ge(back_filled, back_count(b, f"S{j}"))
                        tt(mix[:, 2 * j:2 * j + 2, :], pM[:, :].rearrange("p (c d) -> p c d", c=2),
                           up_const[:, :].unsqueeze(1).broadcast_to([P, 2, D]), ALU.add).then_inc(back_drained, 1)

            def sequence(s, q, first=False, last=False):
                for n in range(NST):
                    if n == 2 and not first:
                        back_step(s - 1, 1 - q, n)
                    scan(s, q, n)
                    for job in EXPERT_STEPS[n]:
                        add_expert(s, q, job)
                    if not last:
                        front_step(s + 1, 1 - q, n)
                    if n != 2 and not first:
                        back_step(s - 1, 1 - q, n)

            nc.vector.memset(ones[:, :], 1.0).then_inc(consts_base, 1)
            nc.vector.memset(eps_c[:, :], EPS).then_inc(consts_base, 1)
            nc.vector.memset(h_pad[:, 0:TAPS - 1], 0.0)
            nc.vector.memset(decay[:, :, :, 0:1], 0.0).then_inc(consts_base, 1)
            dve.wait_ge(w_ready, n_small)
            dve.wait_ge(consts_base, 3)
            dve.wait_ge(consts_ready, 1)
            for t in range(TAPS):
                for half in range(NH):
                    ts(tap_diag[:, t, half, :], ident[:, :], conv_w_c[:, half, t:t + 1], None, ALU.mult).then_inc(
                        taps_diag, 1)
            ts(ln_b_wide[:, :], ones[:, :], ln_b_c[:, :], None, ALU.mult).then_inc(lnb_wide, 1)
            for t in range(TAPS):
                dve.wait_ge(taps_wide, 2 * (t // 2) + 2)
                at = (t % 2) * DIN
                tt(w_conv[:, t, :], w_in[:, 0:DIN], pF[t // 2][:, at:at + DIN], ALU.mult).then_inc(w_made, 1)
            dve.wait_ge(lnb_up, 1)
            tt(up_const[:, :], b_up_r[:, :], pM[:, 0:D], ALU.add).then_inc(w_made, 1)
            ts(w_up_g[:, :], w_up[:, :], ln_g_c[:, :], None, ALU.mult).then_inc(w_made, 1)
            dve.wait_ge(consts_ready, 7)
            dve.wait_ge(w_made, TAPS + 2)
            dve.sem_inc(w_made, 1)
            for n in range(NST):
                front_step(0, 0, n)
            sequence(0, 0, first=True)
            with dve.Fori(1, NSEQ - 1, 2) as s:
                sequence(s, 1)
                sequence(s + 1, 0)
            sequence(NSEQ - 1, 1, last=True)
            for n in range(NST):
                back_step(NSEQ - 1, 1, n)

        @block.gpsimd
        def _(pool):
            tt, copy = nc.gpsimd.tensor_tensor, nc.gpsimd.tensor_copy

            def see(s, n):
                g = s * NST + n
                pool.wait_ge(scanned, g + 1)
                pool.wait_ge(c_copied, g + 1)
                tt(state[:, n % 2, :, :], state[:, n % 2, :, :],
                   c_wide[:, n % 2, :].unsqueeze(1).broadcast_to([P, NH, L]), ALU.mult).then_inc(seen_ready, 1)

            def front_step(f, q, n):
                if n == 8:
                    pool.wait_ge(front_drained, front_count(f, "X"))
                    pool.sem_inc(pool_passed, 1)
                    copy(bc[0:32, q, :], xdbl[0:32, :]).then_inc(split_step, 1)
                    pool.wait_ge(split_step, 4 * f + 1)
                    tt(bc_rest[:, :], xdbl[0:32, :], bc[0:32, q, :], ALU.subtract).then_inc(split_step, 1)
                    pool.wait_ge(split_step, 4 * f + 2)
                    pool.sem_inc(pool_passed, 1)
                    copy(bc_mid[:, :], bc_rest[:, :]).then_inc(split_step, 1)
                    pool.wait_ge(split_step, 4 * f + 3)
                    tt(bc_rest[:, :], bc_rest[:, :], bc_mid[:, :], ALU.subtract).then_inc(split_step, 1)
                if n == 12:
                    pool.wait_ge(onep_ready, f + 1)
                    tt(dt_m[:, :, :], u[:, q, :, :], dt_m[:, :, :], ALU.subtract).then_inc(dt_rest, 1)
                    pool.wait_ge(dt_rest, 2 * f + 1)
                    pool.wait_ge(dt_ln, f + 1)
                    tt(dt_m[:, :, :], dt_m[:, :, :], dt[:, q, :, :], ALU.add).then_inc(dt_rest, 1)
                if n == 13:
                    pool.wait_ge(dt_ready, f + 1)
                    pool.wait_ge(silu_done, f + 1)
                    tt(u[:, q, :, :], dt[:, q, :, :], xz[:, q, 0:NH, :], ALU.mult).then_inc(u_ready, 1)

            def back_step(b, qb, n):
                if n == 2:
                    pool.wait_ge(y_read, b + 1)
                    tt(skip[:, :, :], skip[:, :, :], xz[:, qb, NH:, :], ALU.mult).then_inc(gated, 1)
                if n == 7:
                    pool.wait_ge(back_drained, back_count(b, "S1"))
                    pool.wait_ge(ffn_gate_ready, b + 1)
                    tt(mix, mix, acc[:, qb, :, :], ALU.mult).then_inc(mixed, 1)
                    pool.wait_ge(mixed, b + 1)
                    pool.wait_ge(xres_loaded, 16 * (b + 1))
                    tt(res[:, :, :], res[:, :, :], mix, ALU.add).then_inc(out_ready, 1)

            def sequence(s, q, first=False, last=False):
                for n in range(NST):
                    see(s, n)
                    if not last:
                        front_step(s + 1, 1 - q, n)
                    if not first:
                        back_step(s - 1, 1 - q, n)

            nc.gpsimd.memset(ident[:, :], 0.0).then_inc(consts_pool, 1)
            nc.gpsimd.memset(select[:, :, :], 0.0).then_inc(consts_pool, 1)
            nc.gpsimd.memset(lower[:, :, :], 1.0).then_inc(consts_pool, 1)
            pool.wait_ge(consts_pool, 3)
            nc.gpsimd.affine_select(out=ident[:, :], in_=ident[:, :], compare_op=ALU.not_equal, fill=1.0, base=0,
                                    pattern=[[-1, P]], channel_multiplier=1).then_inc(consts_ready, 1)
            pool.wait_ge(consts_ready, 1)
            pool.sem_inc(consts_ready, 1)
            for part in range(3):
                pool.wait_ge(consts_ready, 2 + part)
                nc.gpsimd.affine_select(out=select[:, :, :], in_=select[:, :, :], compare_op=ALU.not_equal, fill=1.0,
                                        base=-32 * part, pattern=[[-1, 2 * NST], [0, P]],
                                        channel_multiplier=1).then_inc(consts_ready, 1)
            nc.gpsimd.affine_select(out=lower[:, :, :], in_=lower[:, :, :], compare_op=ALU.is_gt, fill=0.0, base=0,
                                    pattern=[[1, E], [-1, E]], channel_multiplier=0).then_inc(consts_ready, 1)
            pool.wait_ge(consts_ready, 6)
            pool.sem_inc(consts_ready, 1)
            for n in range(NST):
                front_step(0, 0, n)
            sequence(0, 0, first=True)
            with pool.Fori(1, NSEQ - 1, 2) as s:
                sequence(s, 1)
                sequence(s + 1, 0)
            sequence(NSEQ - 1, 1, last=True)
            for n in range(NST):
                back_step(NSEQ - 1, 1, n)


_INS = ["L0_attn_x", "L0_attn_W_down", "L0_attn_b_down", "L0_attn_W_in", "L0_attn_conv_w", "L0_attn_conv_b",
        "L0_attn_W_x", "L0_attn_W_dt", "L0_attn_b_dt", "L0_attn_A_log", "L0_attn_D_skip", "L0_attn_W_out",
        "L0_attn_ln_g", "L0_attn_ln_b", "L0_attn_W_up", "L0_attn_b_up", "L0_ffn_gate", "L0_ffn_W1", "L0_ffn_b1",
        "L0_ffn_W2", "L0_ffn_b2"]


def kernel(**inputs):
    import numpy as _np
    import concourse.bacc as _bacc
    from concourse import mybir as _mybir
    from concourse.bass_utils import run_bass_kernel_spmd as _run

    nc = _bacc.Bacc("TRN2", target_bir_lowering=False, num_devices=1)
    arrays, args = {}, []
    for name in _INS:
        a = _np.ascontiguousarray(inputs[name])
        arrays[f"in_{name}_dram"] = a
        args.append(nc.dram_tensor(f"in_{name}_dram", a.shape, _mybir.dt.from_np(a.dtype), kind="ExternalInput").ap())
    args.append(nc.dram_tensor("out_0_dram", (NSEQ, L, D), _mybir.dt.from_np(_np.dtype("float32")),
                               kind="ExternalOutput").ap())
    build(nc, *args)
    r = _run(nc, [arrays], core_ids=[0])
    return r.results[0]["out_0_dram"]
```

```python
from contextlib import ExitStack

import concourse.bass as bass
from concourse import mybir

ALU = mybir.AluOpType
ACT = mybir.ActivationFunctionType
AX = mybir.AxisListType
F32 = mybir.dt.float32
BF16 = mybir.dt.bfloat16
I32 = mybir.dt.int32
U32 = mybir.dt.uint32

P = 128
NSEQ, L, D = 16, 512, 256
TT = L // P
KD = D // P
BD = 128
DIN = 256
NH = DIN // P
NST = 16
TAPS = 4
DTR = 32
E, HID = 8, 512
KH = HID // P
TOP_K = 2
EPS = 1e-5
PAIRS = NST // 2

TOKENS = NSEQ * L
UNIT = 8
NU = TOKENS // (UNIT * P)
RING = 4
ROW = D + 2
SLOTS = 512
ST = SLOTS // P
REGION = TOKENS + SLOTS
NO_TOKEN = float(1 << 20)
TILES = 3 * (NSEQ - 2)
assert TILES >= TOP_K * TOKENS // SLOTS + E
NT = TILES + 1

FRONT = ["V0", "V1", "Z0", "Z1", "X", "D0", "D1"]
FRONT_AT = {4: ["V0"], 5: ["V1"], 6: ["Z0", "Z1"], 9: ["X"], 11: ["D0", "D1"]}
BACK = ["M", "MT", "S0", "S1"]
BACK_AT = {5: ["M"], 7: ["MT"], 8: ["S0", "S1"]}
TILE_JOBS = ["h0", "h1", "h2", "h3", "T0", "T1", "o0", "o1"]


def tile_jobs(q, n):
    m = q * NST + n
    return [(x // 8, TILE_JOBS[x % 8]) for x in range(3 * m // 2, 3 * (m + 1) // 2)]


def build(nc, x, W_down, b_down, W_in, conv_w, conv_b, W_x, W_dt, b_dt, A_log, D_skip, W_out, ln_g, ln_b,
          W_up, b_up, gate, W1, b1, W2, b2, out, slots_dram, f_dram, s_dram):
    with ExitStack() as ctx:
        def sb(name, shape, dt=F32):
            return ctx.enter_context(nc.sbuf_tensor(name, shape, dt))

        def ps(name):
            return ctx.enter_context(nc.psum_tensor(name, [P, 512], F32))

        def sem(name):
            return ctx.enter_context(nc.semaphore(name))

        w_down = sb("w_down", [P, KD, BD])
        w_in = sb("w_in", [P, 2 * DIN])
        w_conv = sb("w_conv", [P, TAPS, DIN])
        w_x = sb("w_x", [P, NH, 2 * NST + DTR])
        w_dt = sb("w_dt", [64, DIN])
        w_out = sb("w_out", [P, NH, BD])
        w_up = sb("w_up", [P, D])
        w_up_g = sb("w_up_g", [P, D])
        w_gate = sb("w_gate", [P, KD, E])
        b1_c = sb("b1_c", [P, E, KH])
        b_down_c = sb("b_down_c", [P, 1])
        conv_w_c = sb("conv_w_c", [P, NH, TAPS])
        conv_b_c = sb("conv_b_c", [P, NH])
        b_dt_c = sb("b_dt_c", [P, NH])
        a_log_c = sb("a_log_c", [P, NH, NST])
        a_exp = sb("a_exp", [P, NH, NST])
        a_neg = sb("a_neg", [P, NH, NST])
        d_skip_c = sb("d_skip_c", [P, NH])
        ln_g_c = sb("ln_g_c", [P, 1])
        ln_b_c = sb("ln_b_c", [P, 1])
        ln_b_wide = sb("ln_b_wide", [P, P])
        up_const = sb("up_const", [P, D])
        ident = sb("ident", [P, P])
        before = sb("before", [P, P])
        ones = sb("ones", [P, P])
        select = sb("select", [96, 2 * NST, P], BF16)
        lower = sb("lower", [P, E, E])
        eps_c = sb("eps_c", [P, 1])

        h_all = sb("h_all", [P, NSEQ, TAPS - 1 + L])
        gate_lo = sb("gate_lo", [P, TOKENS // P])
        gate_hi = sb("gate_hi", [P, TOKENS // P])
        tile_expert = sb("tile_expert", [P, NT])
        tile_table = sb("tile_table", [P, 2, NT], I32)
        list_end = sb("list_end", [P, E], I32)

        shared = sb("shared", [P, 14864])
        taken = 0

        def part(*shape):
            nonlocal taken
            size = 1
            for k in shape:
                size *= k
            flat = shared[:, taken:taken + size]
            taken += size
            names = "abcd"[:len(shape)]
            if len(shape) == 1:
                return flat
            return flat.rearrange(f"p ({' '.join(names)}) -> p {' '.join(names)}",
                                  **{k: v for k, v in list(zip(names, shape))[1:]})

        rows = [part(UNIT, ROW) for _ in range(RING)]
        xnT = [part(KD, UNIT * P) for _ in range(2)]
        above = part(UNIT, E, E)
        equal = part(UNIT, E, E)
        pad_rows = part(ST, ROW)
        taken = 0
        w1 = [part(KD, HID) for _ in range(2)]
        w2 = [part(KH, D) for _ in range(2)]
        slot_rows = [part(ST, ROW) for _ in range(2)]
        slotT = [part(KD, SLOTS) for _ in range(2)]
        hT = [part(KH, SLOTS) for _ in range(2)]
        y_rows = [part(ST, D) for _ in range(2)]
        b2_wide = [part(D) for _ in range(2)]
        taken = 0
        f_rows = [part(TT, 2 * D) for _ in range(2)]
        x_rows = [part(TT, D) for _ in range(2)]
        s_rows = [part(TT, D) for _ in range(2)]
        o_rows = [part(TT, D) for _ in range(2)]
        taken = RING * UNIT * ROW
        tap_diag = part(TAPS, NH, P)

        ln_stats = sb("ln_stats", [P, UNIT, 6])
        ln_mv = sb("ln_mv", [P, UNIT, 2])
        ln_log = sb("ln_log", [P, UNIT])
        ln_rstd = sb("ln_rstd", [P, UNIT])
        logits = sb("logits", [P, UNIT, E])
        lexp = sb("lexp", [P, UNIT, E])
        prob = sb("prob", [P, UNIT, E])
        rank = sb("rank", [P, UNIT, E])
        mask = sb("mask", [P, 2, UNIT, E])
        picked = sb("picked", [P, UNIT, E])
        weight = sb("weight", [P, UNIT, E])
        slot = sb("slot", [P, UNIT, E])
        is_hi = sb("is_hi", [P, UNIT, E])
        w_hi = sb("w_hi", [P, UNIT, E])
        w_lo = sb("w_lo", [P, UNIT, E])
        e_hi = sb("e_hi", [P, UNIT, E])
        small = sb("small", [P, 8, UNIT])
        slot_lo = sb("slot_lo", [P, RING, UNIT], U32)
        slot_hi = sb("slot_hi", [P, RING, UNIT], U32)
        next_slot = sb("next_slot", [P, E])
        iotas_i = sb("iotas_i", [P, 3 * E + 16 + NT], I32)
        iotas = sb("iotas", [P, 3 * E + 16 + NT])
        list_start = iotas[:, 0:E]
        token2 = iotas[:, E:2 * E]
        expert_no = iotas[:, 2 * E:3 * E]
        tile_marks = iotas[:, 3 * E:3 * E + 16]
        tile_no = iotas[:, 3 * E + 16:]
        counts = sb("counts", [P, E])
        tiles_in = sb("tiles_in", [P, E])
        tiles_end = sb("tiles_end", [P, E])
        over_mark = sb("over_mark", [P, E, 16])
        past = sb("past", [P, NT, E])
        tile_first = sb("tile_first", [P, NT])
        tile_row = sb("tile_row", [P, NT])

        xz = sb("xz", [P, 2, 2 * NH, L])
        xdbl = sb("xdbl", [64, L])
        bc = sb("bc", [96, 2, L], BF16)
        bc_rest = sb("bc_rest", [32, L])
        bc_mid = sb("bc_mid", [32, L], BF16)
        dt_v = sb("dt_v", [P, NH, L])
        dt_m = sb("dt_m", [P, NH, L])
        dt = sb("dt", [P, 2, NH, L])
        u_sb = sb("u_sb", [P, 2, NH, L])

        decay = sb("decay", [P, 2, NH, L])
        drive = sb("drive", [P, NH, L])
        state = sb("state", [P, 4, NH, L])
        c_wide = sb("c_wide", [P, 2, L])

        skip = dt_m

        b1_pick = sb("b1_pick", [P, KH, E])
        b1_tile = sb("b1_tile", [P, 2, KH])
        expert_is = sb("expert_is", [P, E])
        is_high = sb("is_high", [P, ST])
        credit = sb("credit", [1, 2, ST])
        y_index = sb("y_index", [P, 2, ST], U32)

        m_sb = dt_m[:, 0, :].rearrange("p (c m) -> p c m", c=TT)
        m_stats = sb("m_stats", [P, TT, 6])
        m_mv = sb("m_mv", [P, TT, 2])
        m_log = sb("m_log", [P, TT])
        m_rstd = sb("m_rstd", [P, TT])
        mnT = dt_m[:, 1, :]
        s_out = sb("s_out", [P, TT, D])

        pB = [ps("pB0"), ps("pB1")]
        pC = ps("pC")
        pY = [ps("pY0"), ps("pY1")]
        pF = [ps("pF0"), ps("pF1")]
        pM = ps("pM")

        w_ready = sem("w_ready")
        b1_ready = sem("b1_ready")
        x_loaded0 = sem("x_loaded0")
        x_loaded1 = sem("x_loaded1")
        x_loaded2 = sem("x_loaded2")
        x_loaded3 = sem("x_loaded3")
        dve_consts = sem("dve_consts")
        pool_memset = sem("pool_memset")
        consts_ready = sem("consts_ready")
        iotas_ready = sem("iotas_ready")
        iotas_float = sem("iotas_float")
        taps_diag = sem("taps_diag")
        taps_wide = sem("taps_wide")
        w_made = sem("w_made")
        lnb_wide = sem("lnb_wide")
        lnb_up = sem("lnb_up")
        a_exp_ready = sem("a_exp_ready")
        a_ready = sem("a_ready")
        r_stats = sem("r_stats")
        r_rstd = sem("r_rstd")
        r_xn = sem("r_xn")
        r_turned = sem("r_turned")
        r_turn_read = sem("r_turn_read")
        r_logits = sem("r_logits")
        r_logits_read = sem("r_logits_read")
        r_h = sem("r_h")
        r_h_read = sem("r_h_read")
        r_step = sem("r_step")
        r_step2 = sem("r_step2")
        r_exp = sem("r_exp")
        r_mask = sem("r_mask")
        r_place = sem("r_place")
        r_place_read = sem("r_place_read")
        r_slots = sem("r_slots")
        r_scattered0 = sem("r_scattered0")
        r_scattered1 = sem("r_scattered1")
        r_scattered2 = sem("r_scattered2")
        r_scattered3 = sem("r_scattered3")
        pads_made = sem("pads_made")
        pads_stored = sem("pads_stored")
        table_step = sem("table_step")
        table_ready = sem("table_ready")
        front_filled = sem("front_filled")
        front_drained = sem("front_drained")
        back_filled = sem("back_filled")
        back_drained = sem("back_drained")
        silu_done = sem("silu_done")
        split_step = sem("split_step")
        bc_shifted = sem("bc_shifted")
        negabs_ready = sem("negabs_ready")
        dt_exp = sem("dt_exp")
        dt_ln = sem("dt_ln")
        onep_ready = sem("onep_ready")
        dt_rest = sem("dt_rest")
        dt_ready = sem("dt_ready")
        u_ready = sem("u_ready")
        b_wide_ready = sem("b_wide_ready")
        c_wide_ready = sem("c_wide_ready")
        c_copied = sem("c_copied")
        decay_ready = sem("decay_ready")
        drive_ready = sem("drive_ready")
        scanned = sem("scanned")
        seen_ready = sem("seen_ready")
        paired = sem("paired")
        summed = sem("summed")
        y_read = sem("y_read")
        gated = sem("gated")
        m_stats_step = sem("m_stats_step")
        m_rstd_step = sem("m_rstd_step")
        mn_ready = sem("mn_ready")
        s_ready = sem("s_ready")
        s_stored = sem("s_stored")
        tile_loaded0 = sem("tile_loaded0")
        tile_loaded1 = sem("tile_loaded1")
        ffn_filled = sem("ffn_filled")
        ffn_free0 = sem("ffn_free0")
        ffn_free1 = sem("ffn_free1")
        b1_step = sem("b1_step")
        b1_tile_ready = sem("b1_tile_ready")
        index_step = sem("index_step")
        index_ready = sem("index_ready")
        y_ready = sem("y_ready")
        y_scattered0 = sem("y_scattered0")
        y_scattered1 = sem("y_scattered1")
        m_loaded0 = sem("m_loaded0")
        m_loaded1 = sem("m_loaded1")
        m_weighted = sem("m_weighted")
        m_added = sem("m_added")
        m_silu = sem("m_silu")
        m_mixed = sem("m_mixed")
        m_out = sem("m_out")
        m_stored0 = sem("m_stored0")
        m_stored1 = sem("m_stored1")
        dve_passed = sem("dve_passed")
        pool_passed = sem("pool_passed")
        act_passed = sem("act_passed")
        x_loaded = [x_loaded0, x_loaded1, x_loaded2, x_loaded3]
        r_scattered = [r_scattered0, r_scattered1, r_scattered2, r_scattered3]
        tile_loaded = [tile_loaded0, tile_loaded1]
        ffn_free = [ffn_free0, ffn_free1]
        y_scattered = [y_scattered0, y_scattered1]
        m_loaded = [m_loaded0, m_loaded1]
        m_stored = [m_stored0, m_stored1]
        def front_count(f, job):
            return f * len(FRONT) + FRONT.index(job) + 1

        def back_count(b, job):
            return b * len(BACK) + BACK.index(job) + 1

        def tile_pos(i, job):
            return 2 + i * len(TILE_JOBS) + TILE_JOBS.index(job) + 1

        def tile_of(k, q, t):
            return 6 * k + 3 * q + t, (q + t) % 2, 3 * k + (3 * q + t) // 2

        def later(s, n, back=4):
            return n >= back or not isinstance(s, int) or s > 0

        x_units = x.rearrange("s l d -> (s l) d").rearrange("(u c p) d -> u p c d", p=P, c=UNIT)
        x_seqs = x.rearrange("s (c p) d -> s p c d", p=P)
        out_seqs = out.rearrange("s (c p) d -> s p c d", p=P)
        s_seqs = s_dram.rearrange("(s c p) d -> s p c d", p=P, c=TT)
        f_seqs = f_dram.rearrange("(s c p two) d -> s p c (two d)", p=P, c=TT, two=2)

        def column(v, n):
            return v.rearrange("(c p) -> p c", p=P) if n > 1 else v.rearrange("(p c) -> p c", c=1)

        small_loads = [
            (w_down[:, :, :], W_down.rearrange("(k p) m -> p k m", p=P)),
            (w_gate[:, :, :], gate.rearrange("(k p) m -> p k m", p=P)),
            (b_down_c[:, :], column(b_down, 1)),
            (w_in[:, :], W_in),
            (conv_w_c[:, :, :], conv_w.rearrange("(c p) k -> p c k", p=P)),
            (w_x[:, :, 0:2 * NST], W_x.rearrange("(k p) m -> p k m", p=P)[:, :, DTR:]),
            (w_x[:, :, 2 * NST:], W_x.rearrange("(k p) m -> p k m", p=P)[:, :, 0:DTR]),
            (w_dt[32:64, :], W_dt),
            (w_out[:, :, :], W_out.rearrange("(k p) m -> p k m", p=P)),
            (w_up[:, :], W_up),
            (conv_b_c[:, :], column(conv_b, NH)),
            (b_dt_c[:, :], column(b_dt, NH)),
            (a_log_c[:, :, :], A_log.rearrange("(c p) n -> p c n", p=P)),
            (d_skip_c[:, :], column(D_skip, NH)),
            (ln_g_c[:, :], column(ln_g, 1)),
            (ln_b_c[:, :], column(ln_b, 1)),
            (up_const[:, :], b_up.partition_broadcast(P)),
        ]
        n_small = 16 * len(small_loads)
        n_consts = 8

        block = ctx.enter_context(nc.Block())

        @block.sync
        def _(sp):
            def load_unit(u):
                if u >= RING:
                    sp.wait_ge(r_scattered[u % RING], 16 * 2 * UNIT * (u // RING))
                sp.dma_start(rows[u % RING][:, :, 0:D], x_units[u]).then_inc(x_loaded[u % RING], 16)

            def load_tile(i, buf):
                row = sp.value_load(tile_table[0:1, 0, bass.ds(i, 1)], min_val=0, max_val=E * REGION)
                e = sp.value_load(tile_table[0:1, 1, bass.ds(i, 1)], min_val=0, max_val=E - 1)
                sp.dma_start(slot_rows[buf], slots_dram[bass.ds(row, SLOTS), :].rearrange(
                    "(c p) w -> p c w", p=P)).then_inc(tile_loaded[buf], 16)
                sp.dma_start(w1[buf], W1[bass.ds(e, 1)].rearrange("o (k p) h -> p (o k) h", p=P)).then_inc(
                    tile_loaded[buf], 16)
                sp.dma_start(w2[buf], W2[bass.ds(e, 1)].rearrange("o (k p) d -> p (o k) d", p=P)).then_inc(
                    tile_loaded[buf], 16)
                sp.dma_start(b2_wide[buf], b2[bass.ds(e, 1)].rearrange("o d -> (o d)").partition_broadcast(P)).then_inc(
                    tile_loaded[buf], 16)

            def next_tile(i, buf):
                sp.wait_ge(y_ready, i - 1)
                load_tile(i, buf)

            def store_s(b):
                sp.wait_ge(s_ready, b + 1)
                sp.dma_start(s_seqs[b], s_out[:, :, :]).then_inc(s_stored, 16)

            def load_mix(d, buf):
                sp.dma_start(f_rows[buf], f_seqs[d]).then_inc(m_loaded[buf], 16)
                sp.dma_start(s_rows[buf], s_seqs[d]).then_inc(m_loaded[buf], 16)
                sp.dma_start(x_rows[buf], x_seqs[d]).then_inc(m_loaded[buf], 16)

            def store_mix(d, buf):
                sp.wait_ge(m_out, d + 1)
                sp.dma_start(out_seqs[d], o_rows[buf]).then_inc(m_stored[buf], 16)

            load_unit(0)
            with nc.allow_non_contiguous_dma(reason="columns of biases, once"):
                for dst, src in small_loads[:3]:
                    sp.dma_start(dst, src).then_inc(w_ready, 16)
                for u in range(1, RING):
                    load_unit(u)
                for dst, src in small_loads[3:]:
                    sp.dma_start(dst, src).then_inc(w_ready, 16)
                sp.dma_start(b1_c[:, :, :], b1.rearrange("e (c p) -> p e c", p=P)).then_inc(b1_ready, 16)
            for u in range(RING, NU):
                load_unit(u)
            sp.wait_ge(pads_made, 2)
            sp.wait_ge(table_ready, 1)
            for e in range(E + 1):
                row = sp.value_load(list_end[0:1, e:e + 1], min_val=0, max_val=E * REGION) if e < E else E * REGION
                sp.dma_start(slots_dram[bass.ds(row, SLOTS), :].rearrange("(c p) w -> p c w", p=P),
                             pad_rows).then_inc(pads_stored, 16)
            sp.wait_ge(pads_stored, 16 * (E + 1))
            for j in range(RING):
                sp.wait_ge(r_scattered[j], 16 * 2 * UNIT * (NU // RING))
            load_tile(0, 0)
            load_tile(1, 1)
            sp.sem_inc(s_stored, 16)
            with sp.Fori(0, NSEQ // 2 - 2) as k:
                for q in range(2):
                    for t in range(3):
                        i, buf, _ = tile_of(k, q, t)
                        next_tile(i + 2, buf)
                    store_s(2 * k + q)
            for q in range(2):
                for t in range(3):
                    i, buf, _ = tile_of(NSEQ // 2 - 2, q, t)
                    if i + 2 < NT:
                        next_tile(i + 2, buf)
                store_s(NSEQ - 4 + q)
            for b in (NSEQ - 2, NSEQ - 1):
                store_s(b)
            sp.wait_ge(s_stored, 16 * (NSEQ + 1))
            for buf in range(2):
                sp.wait_ge(y_scattered[buf], 16 * ST * (TILES // 2 + 1))
            load_mix(0, 0)
            load_mix(1, 1)
            with sp.Fori(0, NSEQ // 2 - 1) as k:
                for buf in range(2):
                    store_mix(2 * k + buf, buf)
                    load_mix(2 * k + buf + 2, buf)
            for buf in range(2):
                store_mix(NSEQ - 2 + buf, buf)
            for buf in range(2):
                sp.wait_ge(m_stored[buf], 16 * NSEQ // 2)

        @block.tensor
        def _(pe):
            mm = nc.tensor.matmul
            turn_banks = [pB[0], pB[1], pC, pY[0]]

            def route_unit(u, j):
                pe.wait_ge(r_xn, u + 1)
                for k in range(KD):
                    for half in range(2):
                        bank = turn_banks[2 * k + half]
                        for c in range(4):
                            last = nc.tensor.transpose(bank[:, c * P:(c + 1) * P],
                                                       rows[j][:, 4 * half + c, k * P:(k + 1) * P], ident[:, :])
                        last.then_inc(r_turned, 1)
                pe.wait_ge(r_turn_read, 4 * u + 4)
                for c in range(UNIT):
                    for k in range(KD):
                        last = mm(pY[1][:, c * E:(c + 1) * E], xnT[j % 2][:, k, c * P:(c + 1) * P], w_gate[:, k, :],
                                  start=(k == 0), stop=(k == KD - 1))
                last.then_inc(r_logits, 1)
                for half in range(2):
                    for k in range(KD):
                        last = mm(pF[half][:, :], w_down[:, k, :], xnT[j % 2][:, k, half * L:(half + 1) * L],
                                  start=(k == 0), stop=(k == KD - 1))
                    last.then_inc(r_h, 1)
                pe.wait_ge(r_mask, u + 1)
                pe.wait_ge(r_h_read, 2 * u + 2)
                picks = mask[:, j % 2, :, :]
                mm(pM[:, 0:UNIT * E], before[:, :], picks.rearrange("p c e -> p (c e)"), start=True, stop=False,
                   skip_group_check=True)
                for c in range(UNIT):
                    if c < UNIT - 1:
                        mm(pM[:, (c + 1) * E:UNIT * E], ones[:, :],
                           picks[:, c, :].unsqueeze(1).broadcast_to([P, UNIT - 1 - c, E]),
                           start=False, stop=False, skip_group_check=True)
                    last = mm(pM[:, UNIT * E:(UNIT + 1) * E], ones[:, :], picks[:, c, :],
                              start=False, stop=(c == UNIT - 1), skip_group_check=True)
                last.then_inc(r_place, 1)

            def spread(s, q, n):
                g = s * NST + n
                if n == 0:
                    pe.wait_ge(split_step, 4 * (s + 1))
                    pe.wait_ge(bc_shifted, 2 * (s + 1))
                if later(s, n, 2):
                    pe.wait_ge(drive_ready, g - 1)
                mm(pB[n % 2][:, :], select[:, n, :], bc[:, q, :], start=True, stop=True).then_inc(b_wide_ready, 1)
                if later(s, n, 1):
                    pe.wait_ge(c_copied, g)
                mm(pC[:, :], select[:, NST + n, :], bc[:, q, :], start=True, stop=True).then_inc(c_wide_ready, 1)

            def add_up(s, pair):
                pe.wait_ge(paired, s * PAIRS + pair + 1)
                if pair == 0 and later(s, 0):
                    pe.wait_ge(y_read, s)
                for half in range(NH):
                    last = mm(pY[half][:, :], ident[:, :], state[:, 2 * pair % 4, half, :],
                              start=(pair == 0), stop=(pair == PAIRS - 1), skip_group_check=True)
                last.then_inc(summed, 1)

            def add_up_at(s, n, first=False):
                if n % 2 == 0 and (n >= 4 or not first):
                    add_up(s if n >= 4 else s - 1, (n - 4) // 2 % PAIRS)

            def front_job(f, q, job, back_done):
                if job != FRONT[0] or later(f, 0):
                    pe.wait_ge(front_drained, front_count(f, job) - 1)
                if back_done is not None:
                    pe.wait_ge(back_drained, back_done)
                i = int(job[1]) if len(job) > 1 else 0
                if job[0] == "V":
                    for t in range(TAPS):
                        last = mm(pM[:, :], w_conv[:, t, i * P:(i + 1) * P], h_all[:, f, t:t + L],
                                  start=(t == 0), stop=(t == TAPS - 1))
                elif job[0] == "Z":
                    last = mm(pM[:, :], w_in[:, DIN + i * P:DIN + (i + 1) * P], h_all[:, f, TAPS - 1:],
                              start=True, stop=True)
                elif job == "X":
                    pe.wait_ge(silu_done, f + 1)
                    for k in range(NH):
                        last = mm(pM[0:64, :], w_x[:, k, :], xz[:, q, k, :], start=(k == 0), stop=(k == NH - 1))
                else:
                    last = mm(pM[:, :], w_dt[32:64, i * P:(i + 1) * P], xdbl[32:64, :], start=True, stop=True)
                last.then_inc(front_filled, 1)

            def back_job(b, job, front_done):
                pe.wait_ge(front_drained, front_done)
                if job != BACK[0]:
                    pe.wait_ge(back_drained, back_count(b, job) - 1)
                if job == "M":
                    pe.wait_ge(gated, b + 1)
                    for c in range(TT):
                        for k in range(NH):
                            last = mm(pM[:, c * BD:(c + 1) * BD], skip[:, k, c * P:(c + 1) * P], w_out[:, k, :],
                                      start=(k == 0), stop=(k == NH - 1))
                elif job == "MT":
                    pe.wait_ge(mn_ready, b + 1)
                    for c in range(TT):
                        last = nc.tensor.transpose(pM[:, c * P:(c + 1) * P], m_sb[:, c, :], ident[:, :])
                else:
                    for c in range(2):
                        t = 2 * int(job[1]) + c
                        last = mm(pM[:, c * D:(c + 1) * D], mnT[:, t * P:(t + 1) * P], w_up_g[:, :],
                                  start=True, stop=True)
                last.then_inc(back_filled, 1)

            def turn_slots(buf):
                for k in range(KD):
                    for c in range(ST):
                        yield k, pF[k][:, c * P:(c + 1) * P], slot_rows[buf][:, c, k * P:(k + 1) * P]

            def expert_job(k, q, t, job):
                i, buf, done = tile_of(k, q, t)
                at = TILE_JOBS.index(job)
                bank, part_no = pF[at % 2], int(job[1])
                pe.wait_ge(ffn_free[at % 2], 1 + 4 * i + at // 2)
                if job == "h0":
                    pe.wait_ge(ffn_free[1], 1 + 4 * i)
                if job == "o0":
                    pe.wait_ge(ffn_free[1], 1 + 4 * i + 2)
                if job[0] == "h":
                    if job == "h0":
                        pe.wait_ge(tile_loaded[buf], 64 * (done + 1))
                    for kk in range(KD):
                        last = mm(bank[:, :], w1[buf][:, kk, part_no * P:(part_no + 1) * P], slotT[buf][:, kk, :],
                                  start=(kk == 0), stop=(kk == KD - 1))
                elif job[0] == "T":
                    pe.wait_ge(tile_loaded[1 - buf], 64 * (done + 1 + buf))
                    for kk, dst, src in turn_slots(1 - buf):
                        if kk == part_no:
                            last = nc.tensor.transpose(dst, src, ident[:, :])
                else:
                    for c in range(2):
                        row_tile = 2 * part_no + c
                        for kk in range(KH):
                            last = mm(bank[:, c * D:(c + 1) * D], hT[buf][:, kk, row_tile * P:(row_tile + 1) * P],
                                      w2[buf][:, kk, :], start=(kk == 0), stop=(kk == KH - 1))
                last.then_inc(ffn_filled, 1)

            def sequence(s, q, k=None, first=False, last=False):
                f_done, b_done = (s + 1) * len(FRONT), None
                for n in range(NST):
                    spread(s, q, n)
                    add_up_at(s, n, first)
                    for job in [] if last else FRONT_AT.get(n, []):
                        front_job(s + 1, 1 - q, job, b_done)
                        f_done = front_count(s + 1, job)
                    for job in [] if first else BACK_AT.get(n, []):
                        back_job(s - 1, job, f_done)
                        b_done = back_count(s - 1, job)
                    if k is not None:
                        for t, job in tile_jobs(1 - q, n):
                            expert_job(k, 1 - q, t % 3, job)

            pe.wait_ge(dve_consts, 4)
            pe.wait_ge(taps_diag, TAPS * NH)
            for t in range(TAPS):
                for half in range(NH):
                    at = (t % 2) * DIN + half * P
                    last = mm(pF[t // 2][:, at:at + P], ones[:, :], tap_diag[:, t, half, :], start=True, stop=True)
                last.then_inc(taps_wide, 1)
            pe.wait_ge(lnb_wide, 1)
            pe.wait_ge(w_ready, n_small)
            mm(pM[:, 0:D], ln_b_wide[:, :], w_up[:, :], start=True, stop=True).then_inc(lnb_up, 1)
            pe.wait_ge(w_made, TAPS + 2)
            pe.wait_ge(consts_ready, n_consts)
            with pe.Fori(0, NU // RING) as lap:
                for j in range(RING):
                    route_unit(lap * RING + j, j)
            pe.wait_ge(r_place_read, 2 * NU)
            pe.wait_ge(r_h_read, 2 * NU)

            for job in FRONT:
                front_job(0, 0, job, None)
            sequence(0, 0, first=True)
            pe.wait_ge(tile_loaded[0], 64)
            for k, dst, src in turn_slots(0):
                ins = nc.tensor.transpose(dst, src, ident[:, :])
                if dst is not None and k == 0:
                    last0 = ins
            last0.then_inc(ffn_filled, 1)
            ins.then_inc(ffn_filled, 1)
            with pe.Fori(0, NSEQ // 2 - 1) as k:
                sequence(2 * k + 1, 1, k)
                sequence(2 * k + 2, 0, k)
            sequence(NSEQ - 1, 1, last=True)
            add_up(NSEQ - 1, PAIRS - 2)
            add_up(NSEQ - 1, PAIRS - 1)
            for job in BACK:
                back_job(NSEQ - 1, job, NSEQ * len(FRONT))

        @block.scalar
        def _(act):
            act_fn, copy = nc.scalar.activation, nc.scalar.copy

            def rstd(count, step, stats, mv, log, dst):
                act.wait_ge(stats, 2 * count)
                act_fn(log, mv[:, :, 1], ACT.Ln, bias=eps_c[:, :]).then_inc(step, 1)
                act.wait_ge(step, 2 * count - 1)
                act_fn(dst, log, ACT.Exp, scale=-0.5).then_inc(step, 1)

            def route_unit(u, j):
                rstd(u + 1, r_rstd, r_stats, ln_mv, ln_log[:, :], ln_rstd[:, :])
                for k in range(KD):
                    for half in range(2):
                        act.wait_ge(r_turned, 4 * u + 2 * k + half + 1)
                        copy(xnT[j % 2][:, k, half * L:(half + 1) * L], [pB[0], pB[1], pC, pY[0]][2 * k + half][:, :]
                             ).then_inc(r_turn_read, 1)
                for half in range(2):
                    act.wait_ge(r_h, 2 * u + half + 1)
                    act.sem_inc(act_passed, 1)
                    act_fn(h_all[:, 2 * u + half, TAPS - 1:], pF[half][:, :], ACT.Identity,
                           bias=b_down_c[:, :]).then_inc(r_h_read, 1)
                act.wait_ge(r_step, 12 * u + 3)
                act_fn(lexp[:, :, :], lexp[:, :, :], ACT.Exp).then_inc(r_exp, 1)

            def c_copy(s, n):
                g = s * NST + n
                act.wait_ge(c_wide_ready, g + 1)
                if later(s, n, 2):
                    act.wait_ge(seen_ready, g - 1)
                copy(c_wide[:, n % 2, :], pC[:, :]).then_inc(c_copied, 1)

            def decays(s, q, n):
                g = s * NST + n
                if n == 0:
                    act.wait_ge(dt_ready, s + 1)
                if later(s, n, 2):
                    act.wait_ge(scanned, g - 1)
                for half in range(NH):
                    last = act_fn(decay[:, n % 2, half, 1:], dt[:, q, half, 1:], ACT.Exp,
                                  scale=a_neg[:, half, n:n + 1])
                last.then_inc(decay_ready, 1)

            def drain_slots(i, job, buf):
                part_no = int(job[1])
                act.wait_ge(ffn_filled, tile_pos(i - 1, job) if not isinstance(i, int) or i > 0 else part_no + 1)
                copy(slotT[buf][:, part_no, :], pF[part_no][:, :]).then_inc(ffn_free[part_no], 1)

            def expert_drain(k, q, t, job):
                i, buf, done = tile_of(k, q, t)
                part_no = int(job[1])
                if job[0] == "h":
                    at = TILE_JOBS.index(job)
                    act.wait_ge(ffn_filled, tile_pos(i, job))
                    if job == "h0":
                        act.wait_ge(b1_tile_ready, i + 1)
                    act_fn(hT[buf][:, part_no, :], pF[at % 2][:, :], ACT.Relu,
                           bias=b1_tile[:, buf, part_no:part_no + 1]).then_inc(ffn_free[at % 2], 1)
                elif job[0] == "T":
                    drain_slots(i + 1, job, 1 - buf)

            def front_drain(f, q, job):
                act.wait_ge(front_filled, front_count(f, job))
                i = int(job[1]) if len(job) > 1 else 0
                if job[0] == "V":
                    if job == "V0" and (not isinstance(f, int) or f > 1):
                        act.wait_ge(gated, f - 1)
                    ins = act_fn(xz[:, q, i, :], pM[:, :], ACT.Identity, bias=conv_b_c[:, i:i + 1])
                elif job[0] == "Z":
                    ins = copy(xz[:, q, NH + i, :], pM[:, :])
                elif job == "X":
                    ins = copy(xdbl[:, :], pM[0:64, :])
                else:
                    ins = act_fn(dt_v[:, i, :], pM[:, :], ACT.Identity, bias=b_dt_c[:, i:i + 1])
                ins.then_inc(front_drained, 1)

            def silu_front(f, q):
                act.wait_ge(front_drained, front_count(f, "Z1"))
                act_fn(xz[:, q, :, :], xz[:, q, :, :], ACT.Silu).then_inc(silu_done, 1)

            def shift_parts(f, q):
                act.wait_ge(split_step, 4 * (f + 1))
                copy(bc[32:64, q, :], bc_mid[:, :]).then_inc(bc_shifted, 1)
                copy(bc[64:96, q, :], bc_rest[:, :]).then_inc(bc_shifted, 1)

            def dt_exps(f, q):
                act.wait_ge(negabs_ready, f + 1)
                act_fn(u_sb[:, q, :, :], dt_m[:, :, :], ACT.Exp).then_inc(dt_exp, 1)
                act.wait_ge(dt_exp, f + 1)
                act_fn(dt[:, q, :, :], u_sb[:, q, :, :], ACT.Ln, bias=1.0).then_inc(dt_ln, 1)

            def back_copy(b, job):
                act.wait_ge(back_filled, back_count(b, job))
                src = pM[:, :].rearrange("p (c m) -> p c m", c=TT) if job == "M" else pM[:, :]
                copy(m_sb if job == "M" else mnT, src).then_inc(back_drained, 1)

            def front_step(f, q, n):
                for job in FRONT_AT.get(n, []):
                    front_drain(f, q, job)
                if n == 7:
                    silu_front(f, q)
                if n == 11:
                    shift_parts(f, q)
                if n == 12:
                    dt_exps(f, q)

            def back_step(b, n):
                if n == 5:
                    back_copy(b, "M")
                if n == 6:
                    rstd(b + 1, m_rstd_step, m_stats_step, m_mv, m_log[:, :], m_rstd[:, :])
                if n == 7:
                    back_copy(b, "MT")

            def sequence(s, q, k=None, first=False, last=False):
                for n in range(NST):
                    c_copy(s, n)
                    decays(s, q, n)
                    if not last:
                        front_step(s + 1, 1 - q, n)
                    if not first:
                        back_step(s - 1, n)
                    if k is not None:
                        for t, job in tile_jobs(1 - q, n):
                            expert_drain(k, 1 - q, t % 3, job)

            act.wait_ge(w_ready, n_small)
            act_fn(a_exp[:, :, :], a_log_c[:, :, :], ACT.Exp).then_inc(a_exp_ready, 1)
            act.wait_ge(a_exp_ready, 1)
            nc.scalar.mul(a_neg[:, :, :], a_exp[:, :, :], -1.0).then_inc(a_ready, 1)
            act.wait_ge(a_ready, 1)
            act.wait_ge(dve_consts, 4)
            with act.Fori(0, NU // RING) as lap:
                for j in range(RING):
                    route_unit(lap * RING + j, j)
            for n in range(NST):
                front_step(0, 0, n)
            sequence(0, 0, first=True)
            for job in ("T0", "T1"):
                drain_slots(0, job, 0)
            with act.Fori(0, NSEQ // 2 - 1) as k:
                sequence(2 * k + 1, 1, k)
                sequence(2 * k + 2, 0, k)
            sequence(NSEQ - 1, 1, last=True)
            for n in range(NST):
                back_step(NSEQ - 1, n)

            def silu_mix(d, buf):
                act.wait_ge(m_added, d + 1)
                act_fn(f_rows[buf][:, :, 0:D], f_rows[buf][:, :, 0:D], ACT.Silu).then_inc(m_silu, 1)

            with act.Fori(0, NSEQ // 2) as k:
                for buf in range(2):
                    silu_mix(2 * k + buf, buf)

        @block.vector
        def _(dve):
            tt, ts, stt = nc.vector.tensor_tensor, nc.vector.tensor_scalar, nc.vector.scalar_tensor_tensor
            reduce, vcopy = nc.vector.tensor_reduce, nc.vector.tensor_copy

            def statistics(count, step, n, src, stats, mv):
                for c in range(n):
                    last = nc.vector.bn_stats(stats[:, c, :], src(c))
                last.then_inc(step, 1)
                dve.wait_ge(step, 2 * count - 1)
                dve.sem_inc(dve_passed, 1)
                for c in range(n):
                    last = nc.vector.bn_aggr(mv[:, c, :], stats[:, c, :])
                last.then_inc(step, 1)
                dve.wait_ge(step, 2 * count)

            def normalise_unit(u, j):
                dve.wait_ge(x_loaded[j], 16 * (u // RING + 1) if isinstance(u, int) else 16 * laps)
                statistics(u + 1, r_stats, UNIT, lambda c: rows[j][:, c, 0:D], ln_stats, ln_mv)
                dve.wait_ge(r_rstd, 2 * (u + 1))
                for c in range(UNIT):
                    last = ts(rows[j][:, c, 0:D], rows[j][:, c, 0:D], ln_mv[:, c, 0:1], ln_rstd[:, c:c + 1],
                              ALU.subtract, ALU.mult)
                last.then_inc(r_xn, 1)

            def wide(v):
                return v.unsqueeze(2).broadcast_to([P, UNIT, E])

            def route_unit(u, j):
                lmax, lsum, linv, psum_k, guarded, pinv, hi, both = (small[:, i, :] for i in range(8))
                count = 12 * u

                def step(ins):
                    nonlocal count
                    ins.then_inc(r_step, 1)
                    count = count + 1
                    dve.wait_ge(r_step, count)

                dve.wait_ge(r_logits, u + 1)
                step(vcopy(logits[:, :, :], pY[1][:, 0:UNIT * E].rearrange("p (c e) -> p c e", c=UNIT)))
                step(reduce(lmax, logits[:, :, :], AX.X, ALU.max))
                step(tt(lexp[:, :, :], logits[:, :, :], wide(lmax), ALU.subtract))
                dve.wait_ge(r_exp, u + 1)
                step(reduce(lsum, lexp[:, :, :], AX.X, ALU.add))
                step(nc.vector.reciprocal(linv, lsum))
                step(tt(prob[:, :, :], lexp[:, :, :], wide(linv), ALU.mult))
                rivals = prob[:, :, :].unsqueeze(2).broadcast_to([P, UNIT, E, E])
                own = prob[:, :, :].unsqueeze(3).broadcast_to([P, UNIT, E, E])
                tt(above, rivals, own, ALU.is_gt)
                step(tt(equal, rivals, own, ALU.is_equal))
                low = lower[:, :, :].rearrange("p i j -> p (i j)").unsqueeze(1).broadcast_to([P, UNIT, E * E])
                flat = "p c i j -> p c (i j)"
                step(tt(equal.rearrange(flat), equal.rearrange(flat), low, ALU.mult))
                step(tt(above, above, equal, ALU.add))
                step(reduce(rank[:, :, :], above, AX.X, ALU.add))
                ts(mask[:, j % 2, :, :], rank[:, :, :], float(TOP_K), None, ALU.is_lt).then_inc(r_mask, 1)
                dve.wait_ge(r_mask, u + 1)
                step(tt(picked[:, :, :], mask[:, j % 2, :, :], prob[:, :, :], ALU.mult))
                step(reduce(psum_k, picked[:, :, :], AX.X, ALU.add))

                count = 13 * u

                def step2(ins):
                    nonlocal count
                    ins.then_inc(r_step2, 1)
                    count = count + 1
                    dve.wait_ge(r_step2, count)

                step2(ts(guarded, psum_k, 1e-12, None, ALU.max))
                step2(nc.vector.reciprocal(pinv, guarded))
                tt(weight[:, :, :], picked[:, :, :], wide(pinv), ALU.mult)
                dve.wait_ge(r_place, u + 1)
                tt(slot[:, :, :], pM[:, 0:UNIT * E].rearrange("p (c e) -> p c e", c=UNIT),
                   next_slot[:, :].unsqueeze(1).broadcast_to([P, UNIT, E]), ALU.add).then_inc(r_place_read, 1)
                dve.wait_ge(r_place_read, 2 * u + 1)
                step2(tt(next_slot[:, :], pM[:, UNIT * E:(UNIT + 1) * E], next_slot[:, :], ALU.add))
                dve.sem_inc(r_place_read, 1)
                step2(tt(slot[:, :, :], slot[:, :, :], mask[:, j % 2, :, :], ALU.mult))
                reduce(both, slot[:, :, :], AX.X, ALU.add)
                step2(reduce(hi, slot[:, :, :], AX.X, ALU.max))
                tt(slot_lo[:, j, :], both, hi, ALU.subtract)
                vcopy(slot_hi[:, j, :], hi)
                step2(tt(is_hi[:, :, :], slot[:, :, :], wide(hi), ALU.is_equal))
                tt(e_hi[:, :, :], is_hi[:, :, :], expert_no.unsqueeze(1).broadcast_to([P, UNIT, E]), ALU.mult)
                step2(tt(w_hi[:, :, :], is_hi[:, :, :], weight[:, :, :], ALU.mult))
                step2(tt(w_lo[:, :, :], weight[:, :, :], w_hi[:, :, :], ALU.subtract))
                step2(vcopy(rows[j][:, :, D], token2))
                step2(ts(token2, token2, float(2 * UNIT * P), None, ALU.add))
                step2(reduce(rows[j][:, :, D + 1], e_hi[:, :, :], AX.X, ALU.add))
                step2(reduce(gate_hi[:, bass.ds(u * UNIT, UNIT)], w_hi[:, :, :], AX.X, ALU.add))
                step2(reduce(gate_lo[:, bass.ds(u * UNIT, UNIT)], w_lo[:, :, :], AX.X, ALU.add))
                dve.sem_inc(r_slots, 1)

            def make_table():
                count = 0

                def step(ins):
                    nonlocal count
                    ins.then_inc(table_step, 1)
                    count += 1
                    dve.wait_ge(table_step, count)

                def tiles_by(v):
                    return v.unsqueeze(1).broadcast_to([P, NT, E])

                step(tt(counts[:, :], next_slot[:, :], list_start, ALU.subtract))
                step(tt(over_mark[:, :, :], counts[:, :].unsqueeze(2).broadcast_to([P, E, 16]),
                        tile_marks.unsqueeze(1).broadcast_to([P, E, 16]), ALU.is_gt))
                step(reduce(tiles_in[:, :], over_mark[:, :, :], AX.X, ALU.add))
                step(nc.vector.tensor_tensor_scan(tiles_end[:, :], ones[:, 0:E], tiles_in[:, :], 0.0,
                                                  ALU.mult, ALU.add))
                step(tt(past[:, :, :], tile_no.unsqueeze(2).broadcast_to([P, NT, E]), tiles_by(tiles_end[:, :]),
                        ALU.is_ge))
                step(reduce(tile_expert[:, :], past[:, :, :], AX.X, ALU.add))
                step(tt(past[:, :, :], past[:, :, :], tiles_by(tiles_end[:, :]), ALU.mult))
                step(reduce(tile_first[:, :], past[:, :, :], AX.X, ALU.max))
                step(tt(tile_row[:, :], tile_no, tile_first[:, :], ALU.subtract))
                step(ts(tile_row[:, :], tile_row[:, :], float(SLOTS), None, ALU.mult))
                step(stt(tile_row[:, :], tile_expert[:, :], float(REGION), tile_row[:, :], ALU.mult, ALU.add))
                step(ts(tile_table[:, 0, :], tile_row[:, :], float(E * REGION), None, ALU.min))
                step(ts(tile_expert[:, :], tile_expert[:, :], float(E - 1), None, ALU.min))
                step(vcopy(tile_table[:, 1, :], tile_expert[:, :]))
                step(vcopy(list_end[:, :], next_slot[:, :]))
                dve.sem_inc(table_ready, 1)

            def pair_up(s, pair):
                dve.wait_ge(seen_ready, s * NST + 2 * pair + 2)
                a = 2 * pair % 4
                tt(state[:, a, :, :], state[:, a, :, :], state[:, a + 1, :, :], ALU.add).then_inc(paired, 1)

            def pair_up_at(s, n, first=False):
                if n % 2 == 1 and (n >= 3 or not first):
                    pair_up(s if n >= 3 else s - 1, (n - 3) // 2 % PAIRS)

            def scan(s, q, n):
                g = s * NST + n
                dve.wait_ge(b_wide_ready, g + 1)
                if n == 0:
                    dve.wait_ge(u_ready, s + 1)
                if later(s, n, 1):
                    dve.wait_ge(scanned, g)
                tt(drive[:, :, :], u_sb[:, q, :, :],
                   pB[n % 2][:, :].unsqueeze(1).broadcast_to([P, NH, L]), ALU.mult).then_inc(drive_ready, 1)
                dve.wait_ge(drive_ready, g + 1)
                dve.wait_ge(decay_ready, g + 1)
                if later(s, n, 4):
                    if n % 2 == 0:
                        dve.wait_ge(summed, s * PAIRS + n // 2 - 1)
                    else:
                        dve.wait_ge(paired, s * PAIRS + (n - 1) // 2 - 1)
                flat = "p h t -> p (h t)"
                nc.vector.tensor_tensor_scan(state[:, n % 4, :, :].rearrange(flat),
                                             decay[:, n % 2, :, :].rearrange(flat),
                                             drive[:, :, :].rearrange(flat),
                                             0.0, ALU.mult, ALU.add).then_inc(scanned, 1)

            def pick_bias(i, buf):
                dve.wait_ge(b1_ready, 16)
                ts(expert_is[:, :], expert_no, tile_expert[:, bass.ds(i, 1)], None, ALU.is_equal).then_inc(b1_step, 1)
                dve.wait_ge(b1_step, 2 * i + 1)
                tt(b1_pick[:, :, :], b1_c[:, :, :].rearrange("p e c -> p c e"),
                   expert_is[:, :].unsqueeze(1).broadcast_to([P, KH, E]), ALU.mult).then_inc(b1_step, 1)
                dve.wait_ge(b1_step, 2 * i + 2)
                reduce(b1_tile[:, buf, :], b1_pick[:, :, :], AX.X, ALU.add).then_inc(b1_tile_ready, 1)

            def expert_drain(k, q, t, job):
                i, buf, done = tile_of(k, q, t)
                if job == "T0":
                    pick_bias(i + 1, 1 - buf)
                if job[0] != "o":
                    return
                at, part_no = TILE_JOBS.index(job), int(job[1])
                if job == "o0":
                    dve.wait_ge(y_scattered[buf], 16 * ST * (done + 1))
                    dve.wait_ge(tile_loaded[buf], 64 * (done + 1))
                    ts(is_high[:, :], slot_rows[buf][:, :, D + 1], tile_expert[:, bass.ds(i, 1)], None,
                       ALU.is_equal).then_inc(index_step, 1)
                    dve.wait_ge(index_step, i + 1)
                    tt(y_index[:, buf, :], slot_rows[buf][:, :, D], is_high[:, :], ALU.add).then_inc(index_ready, 1)
                dve.wait_ge(ffn_filled, tile_pos(i, job))
                tt(y_rows[buf][:, 2 * part_no:2 * part_no + 2, :], pF[at % 2][:, :].rearrange("p (c d) -> p c d", c=2),
                   b2_wide[buf].unsqueeze(1).broadcast_to([P, 2, D]), ALU.add).then_inc(ffn_free[at % 2], 1)
                if job == "o1":
                    dve.wait_ge(ffn_free[1], 1 + 4 * i + at // 2 + 1)
                    dve.wait_ge(ffn_free[0], 1 + 4 * i + at // 2 + 1)
                    dve.sem_inc(y_ready, 1)

            def front_step(f, q, n):
                if n == 12:
                    dve.wait_ge(front_drained, front_count(f, "D1"))
                    if later(f, 0):
                        dve.wait_ge(u_ready, f)
                    stt(dt_m[:, :, :], dt_v[:, :, :], -1.0, dt_v[:, :, :], ALU.mult, ALU.min).then_inc(
                        negabs_ready, 1)
                if n == 13:
                    dve.wait_ge(dt_exp, f + 1)
                    ts(dt_m[:, :, :], u_sb[:, q, :, :], 1.0, 1.0, ALU.add, ALU.subtract).then_inc(onep_ready, 1)
                if n == 14:
                    dve.wait_ge(dt_rest, 2 * (f + 1))
                    stt(dt[:, q, :, :], dt_v[:, :, :], 0.0, dt_m[:, :, :], ALU.max, ALU.add).then_inc(dt_ready, 1)

            def skip_term(b, qb):
                dve.wait_ge(summed, PAIRS * (b + 1))
                for half in range(NH):
                    last = stt(skip[:, half, :], xz[:, qb, half, :], d_skip_c[:, half:half + 1],
                               pY[half][:, :], ALU.mult, ALU.add)
                last.then_inc(y_read, 1)

            def back_step(b, n):
                if n == 6:
                    dve.wait_ge(back_drained, back_count(b, "M"))
                    statistics(b + 1, m_stats_step, TT, lambda c: m_sb[:, c, :], m_stats, m_mv)
                    dve.wait_ge(m_rstd_step, 2 * (b + 1))
                    for c in range(TT):
                        last = ts(m_sb[:, c, :], m_sb[:, c, :], m_mv[:, c, 0:1], m_rstd[:, c:c + 1],
                                  ALU.subtract, ALU.mult)
                    last.then_inc(mn_ready, 1)
                if n == 8:
                    dve.wait_ge(s_stored, 16 * (b + 1))
                    for j in range(2):
                        dve.wait_ge(back_filled, back_count(b, f"S{j}"))
                        tt(s_out[:, 2 * j:2 * j + 2, :], pM[:, :].rearrange("p (c d) -> p c d", c=2),
                           up_const[:, :].unsqueeze(1).broadcast_to([P, 2, D]), ALU.add).then_inc(back_drained, 1)
                    dve.wait_ge(back_drained, back_count(b, "S1"))
                    dve.sem_inc(s_ready, 1)

            def sequence(s, q, k=None, first=False, last=False):
                for n in range(NST):
                    pair_up_at(s, n, first)
                    if n == 3 and not first:
                        skip_term(s - 1, 1 - q)
                    scan(s, q, n)
                    if not last:
                        front_step(s + 1, 1 - q, n)
                    if not first:
                        back_step(s - 1, n)
                    if k is not None:
                        for t, job in tile_jobs(1 - q, n):
                            expert_drain(k, 1 - q, t % 3, job)

            nc.vector.memset(ones[:, :], 1.0).then_inc(dve_consts, 1)
            nc.vector.memset(eps_c[:, :], EPS).then_inc(dve_consts, 1)
            nc.vector.memset(h_all[:, :, 0:TAPS - 1], 0.0).then_inc(dve_consts, 1)
            nc.vector.memset(decay[:, :, :, 0:1], 0.0).then_inc(dve_consts, 1)
            dve.wait_ge(w_ready, n_small)
            dve.wait_ge(dve_consts, 4)
            dve.wait_ge(consts_ready, n_consts)
            vcopy(iotas[:, :], iotas_i[:, :]).then_inc(iotas_float, 1)
            for t in range(TAPS):
                for half in range(NH):
                    ts(tap_diag[:, t, half, :], ident[:, :], conv_w_c[:, half, t:t + 1], None, ALU.mult).then_inc(
                        taps_diag, 1)
            ts(ln_b_wide[:, :], ones[:, :], ln_b_c[:, :], None, ALU.mult).then_inc(lnb_wide, 1)
            for t in range(TAPS):
                dve.wait_ge(taps_wide, 2 * (t // 2) + 2)
                at = (t % 2) * DIN
                tt(w_conv[:, t, :], w_in[:, 0:DIN], pF[t // 2][:, at:at + DIN], ALU.mult).then_inc(w_made, 1)
            dve.wait_ge(lnb_up, 1)
            tt(up_const[:, :], up_const[:, :], pM[:, 0:D], ALU.add).then_inc(w_made, 1)
            ts(w_up_g[:, :], w_up[:, :], ln_g_c[:, :], None, ALU.mult).then_inc(w_made, 1)
            dve.wait_ge(w_made, TAPS + 2)
            dve.wait_ge(iotas_float, 1)
            vcopy(next_slot[:, :], list_start).then_inc(iotas_float, 1)
            nc.vector.memset(pad_rows, 0.0).then_inc(pads_made, 1)
            dve.wait_ge(pads_made, 1)
            nc.vector.memset(pad_rows[:, :, D], NO_TOKEN).then_inc(pads_made, 1)
            dve.wait_ge(iotas_float, 2)

            with dve.Fori(0, NU // RING) as lap:
                laps = lap + 1
                for j in range(RING):
                    normalise_unit(lap * RING + j, j)
                    route_unit(lap * RING + j, j)
            make_table()
            for n in range(NST):
                front_step(0, 0, n)
            sequence(0, 0, first=True)
            pick_bias(0, 0)
            with dve.Fori(0, NSEQ // 2 - 1) as k:
                sequence(2 * k + 1, 1, k)
                sequence(2 * k + 2, 0, k)
            sequence(NSEQ - 1, 1, last=True)
            pair_up(NSEQ - 1, PAIRS - 1)
            skip_term(NSEQ - 1, 1)
            for n in range(NST):
                back_step(NSEQ - 1, n)

            def mix(d, k, buf):
                dve.wait_ge(m_loaded[buf], 48 * (k + 1))
                both = f_rows[buf]
                for c in range(TT):
                    last = ts(both[:, c, 0:D], both[:, c, 0:D], gate_lo[:, bass.ds(d * TT + c, 1)], None, ALU.mult)
                last.then_inc(m_weighted, 1)
                dve.wait_ge(m_weighted, d + 1)
                for c in range(TT):
                    last = stt(both[:, c, 0:D], both[:, c, D:], gate_hi[:, bass.ds(d * TT + c, 1)], both[:, c, 0:D],
                               ALU.mult, ALU.add)
                last.then_inc(m_added, 1)

            def finish(d, k, buf, stored):
                if stored:
                    dve.wait_ge(m_stored[buf], 16 * k)
                dve.wait_ge(m_mixed, d + 1)
                tt(o_rows[buf], s_rows[buf], x_rows[buf], ALU.add).then_inc(m_out, 1)

            for buf in range(2):
                mix(buf, 0, buf)
                finish(buf, 0, buf, False)
            with dve.Fori(1, NSEQ // 2) as k:
                for buf in range(2):
                    mix(2 * k + buf, k, buf)
                    finish(2 * k + buf, k, buf, True)

        @block.gpsimd
        def _(pool):
            tt, copy = nc.gpsimd.tensor_tensor, nc.gpsimd.tensor_copy

            def scatter_unit(u, j):
                pool.wait_ge(r_slots, u + 1)
                pool.sem_inc(pool_passed, 1)
                for c in range(UNIT):
                    for index in (slot_lo, slot_hi):
                        nc.gpsimd.indirect_dma_start(
                            slots_dram, bass.IndirectOffsetOnAxis(ap=index[:, j, c:c + 1], axis=0),
                            rows[j][:, c, :], None).then_inc(r_scattered[j], 16)

            def scatter_tile(k, q, t):
                i, buf, done = tile_of(k, q, t)
                pool.wait_ge(index_ready, i + 1)
                pool.wait_ge(y_ready, i + 1)
                pool.sem_inc(pool_passed, 1)
                for c in range(ST):
                    nc.gpsimd.indirect_dma_start(
                        f_dram, bass.IndirectOffsetOnAxis(ap=y_index[:, buf, c:c + 1], axis=0),
                        y_rows[buf][:, c, :], None, bounds_check=2 * TOKENS - 1,
                        oob_is_err=False).then_inc(y_scattered[buf], 16)

            def see(s, n):
                g = s * NST + n
                pool.wait_ge(scanned, g + 1)
                pool.wait_ge(c_copied, g + 1)
                tt(state[:, n % 4, :, :], state[:, n % 4, :, :],
                   c_wide[:, n % 2, :].unsqueeze(1).broadcast_to([P, NH, L]), ALU.mult).then_inc(seen_ready, 1)

            def front_step(f, q, n):
                if n == 10:
                    pool.wait_ge(front_drained, front_count(f, "X"))
                    pool.sem_inc(pool_passed, 1)
                    copy(bc[0:32, q, :], xdbl[0:32, :]).then_inc(split_step, 1)
                    pool.wait_ge(split_step, 4 * f + 1)
                    tt(bc_rest[:, :], xdbl[0:32, :], bc[0:32, q, :], ALU.subtract).then_inc(split_step, 1)
                    pool.wait_ge(split_step, 4 * f + 2)
                    pool.sem_inc(pool_passed, 1)
                    copy(bc_mid[:, :], bc_rest[:, :]).then_inc(split_step, 1)
                    pool.wait_ge(split_step, 4 * f + 3)
                    tt(bc_rest[:, :], bc_rest[:, :], bc_mid[:, :], ALU.subtract).then_inc(split_step, 1)
                if n == 13:
                    pool.wait_ge(onep_ready, f + 1)
                    tt(dt_m[:, :, :], u_sb[:, q, :, :], dt_m[:, :, :], ALU.subtract).then_inc(dt_rest, 1)
                    pool.wait_ge(dt_rest, 2 * f + 1)
                    pool.wait_ge(dt_ln, f + 1)
                    tt(dt_m[:, :, :], dt_m[:, :, :], dt[:, q, :, :], ALU.add).then_inc(dt_rest, 1)
                if n == 14:
                    pool.wait_ge(dt_ready, f + 1)
                    pool.wait_ge(silu_done, f + 1)
                    tt(u_sb[:, q, :, :], dt[:, q, :, :], xz[:, q, 0:NH, :], ALU.mult).then_inc(u_ready, 1)

            def gate_y(b, qb):
                pool.wait_ge(y_read, b + 1)
                tt(skip[:, :, :], skip[:, :, :], xz[:, qb, NH:, :], ALU.mult).then_inc(gated, 1)

            def sequence(s, q, k=None, first=False, last=False):
                for n in range(NST):
                    if n == 3 and not first:
                        gate_y(s - 1, 1 - q)
                    see(s, n)
                    if not last:
                        front_step(s + 1, 1 - q, n)
                    if k is not None:
                        for t, job in tile_jobs(1 - q, n):
                            if job == "o1":
                                scatter_tile(k, 1 - q, t % 3)

            nc.gpsimd.memset(ident[:, :], 0.0).then_inc(pool_memset, 1)
            nc.gpsimd.memset(before[:, :], 1.0).then_inc(pool_memset, 1)
            nc.gpsimd.memset(select[:, :, :], 0.0).then_inc(pool_memset, 1)
            nc.gpsimd.memset(lower[:, :, :], 1.0).then_inc(pool_memset, 1)
            pool.wait_ge(pool_memset, 4)
            nc.gpsimd.affine_select(out=ident[:, :], in_=ident[:, :], compare_op=ALU.not_equal, fill=1.0, base=0,
                                    pattern=[[-1, P]], channel_multiplier=1).then_inc(consts_ready, 1)
            nc.gpsimd.affine_select(out=before[:, :], in_=before[:, :], compare_op=ALU.is_gt, fill=0.0, base=0,
                                    pattern=[[1, P]], channel_multiplier=-1).then_inc(consts_ready, 1)
            for part_no in range(3):
                pool.wait_ge(consts_ready, 2 + part_no)
                nc.gpsimd.affine_select(out=select[:, :, :], in_=select[:, :, :], compare_op=ALU.not_equal, fill=1.0,
                                        base=-32 * part_no, pattern=[[-1, 2 * NST], [0, P]],
                                        channel_multiplier=1).then_inc(consts_ready, 1)
            nc.gpsimd.affine_select(out=lower[:, :, :], in_=lower[:, :, :], compare_op=ALU.is_gt, fill=0.0, base=0,
                                    pattern=[[1, E], [-1, E]], channel_multiplier=0).then_inc(consts_ready, 1)
            at = 0
            for width, step, per_partition in ((E, REGION, 0), (E, 2 * P, 2), (E, 1, 0), (16, SLOTS, 0), (NT, 1, 0)):
                ins = nc.gpsimd.iota(iotas_i[:, at:at + width], pattern=[[step, width]], base=0,
                                     channel_multiplier=per_partition)
                ins.then_inc(iotas_ready, 1)
                at += width
            pool.wait_ge(consts_ready, 6)
            pool.wait_ge(iotas_ready, 5)
            pool.sem_inc(consts_ready, 2)

            pool.wait_ge(dve_consts, 2)
            for buf in range(2):
                for c in range(ST):
                    pool.dma_start(credit[0:1, buf, c:c + 1], eps_c[0:1, :]).then_inc(y_scattered[buf], 16)

            with pool.Fori(0, NU // RING) as lap:
                for j in range(RING):
                    scatter_unit(lap * RING + j, j)
            for n in range(NST):
                front_step(0, 0, n)
            sequence(0, 0, first=True)
            with pool.Fori(0, NSEQ // 2 - 1) as k:
                sequence(2 * k + 1, 1, k)
                sequence(2 * k + 2, 0, k)
            sequence(NSEQ - 1, 1, last=True)
            gate_y(NSEQ - 1, 1)

            def mix(d, buf):
                pool.wait_ge(m_silu, d + 1)
                tt(s_rows[buf], s_rows[buf], f_rows[buf][:, :, 0:D], ALU.mult).then_inc(m_mixed, 1)

            with pool.Fori(0, NSEQ // 2) as k:
                for buf in range(2):
                    mix(2 * k + buf, buf)


_INS = ["L0_attn_x", "L0_attn_W_down", "L0_attn_b_down", "L0_attn_W_in", "L0_attn_conv_w", "L0_attn_conv_b",
        "L0_attn_W_x", "L0_attn_W_dt", "L0_attn_b_dt", "L0_attn_A_log", "L0_attn_D_skip", "L0_attn_W_out",
        "L0_attn_ln_g", "L0_attn_ln_b", "L0_attn_W_up", "L0_attn_b_up", "L0_ffn_gate", "L0_ffn_W1", "L0_ffn_b1",
        "L0_ffn_W2", "L0_ffn_b2"]


def kernel(**inputs):
    import numpy as _np
    import concourse.bacc as _bacc
    from concourse import mybir as _mybir
    from concourse.bass_utils import run_bass_kernel_spmd as _run

    nc = _bacc.Bacc("TRN2", target_bir_lowering=False, num_devices=1)
    arrays, args = {}, []
    for name in _INS:
        a = _np.ascontiguousarray(inputs[name])
        arrays[f"in_{name}_dram"] = a
        args.append(nc.dram_tensor(f"in_{name}_dram", a.shape, _mybir.dt.from_np(a.dtype), kind="ExternalInput").ap())
    args.append(nc.dram_tensor("out_0_dram", (NSEQ, L, D), _mybir.dt.from_np(_np.dtype("float32")),
                               kind="ExternalOutput").ap())
    f32 = _mybir.dt.from_np(_np.dtype("float32"))
    args.append(nc.dram_tensor("slots_dram", (E * REGION + SLOTS, ROW), f32).ap())
    args.append(nc.dram_tensor("f_dram", (TOP_K * TOKENS, D), f32).ap())
    args.append(nc.dram_tensor("s_dram", (TOKENS, D), f32).ap())
    build(nc, *args)
    r = _run(nc, [arrays], core_ids=[0])
    return r.results[0]["out_0_dram"]
```

```python
from contextlib import ExitStack

import concourse.bass as bass
from concourse import mybir

ALU = mybir.AluOpType
ACT = mybir.ActivationFunctionType
AX = mybir.AxisListType
F32 = mybir.dt.float32
BF16 = mybir.dt.bfloat16
I32 = mybir.dt.int32
U32 = mybir.dt.uint32

P = 128
NSEQ, L, D = 16, 512, 256
TT = L // P
KD = D // P
BD = 128
DIN = 256
NH = DIN // P
NST = 16
TAPS = 4
DTR = 32
E, HID = 8, 512
KH = HID // P
TOP_K = 2
EPS = 1e-5
PAIRS = NST // 2

TOKENS = NSEQ * L
UNIT = 8
NU = TOKENS // (UNIT * P)
RING = 4
ROW = D + 2
SLOTS = 512
ST = SLOTS // P
REGION = TOKENS + SLOTS
NO_TOKEN = float(1 << 20)
TILE_PAIRS = 6
TILES = 3 * (2 * TILE_PAIRS + 1)
assert TILES >= (TOP_K * TOKENS + E * (SLOTS - 1)) // SLOTS
NT = TILES + 1

FRONT = ["V0", "V1", "Z0", "Z1", "X", "D0", "D1"]
BACK = ["M", "MT", "S0", "S1"]
JOB_AT = {(2, 0): "V0", (3, 0): "V1", (5, 0): "Z0", (6, 0): "Z1", (7, 0): "M", (8, 0): "X", (9, 0): "D0",
          (9, 1): "D1", (10, 0): "MT", (10, 1): "S0", (11, 0): "S1"}
STATES = 8
C_COPIES = 4
LAST_SUM = 4


def together(s):
    return 1 if isinstance(s, int) and s >= NSEQ - 2 else 4


def sums_before(s):
    per_sequence = NST // 4
    return per_sequence * s if not isinstance(s, int) else sum(NST // together(b) for b in range(s))


def groups_at(s, n, lag):
    due = []
    for b, m in ((s - 1, n + NST), (s, n)):
        size = together(b)
        if size in lag and (not isinstance(b, int) or b >= 0):
            group, rest = divmod(m - lag[size], size)
            if rest == 0 and 0 <= group < NST // size:
                due.append((b, group))
    return due


PAIR_LAG = {4: 4}, {4: 6}
FOUR_LAG = {4: 6}
SUM_LAG = {4: 8, 1: 5}


TILE_JOBS = ["h0", "h1", "h2", "h3", "T0", "T1", "o0", "o1"]


def tile_jobs(q, n):
    m = q * NST + n
    return [(x // 8, TILE_JOBS[x % 8]) for x in range(3 * m // 2, 3 * (m + 1) // 2)]


MIXED = 4
MIX_AT = {}
for d in range(NSEQ):
    start = 4 + 4 * (d // 2)
    for stage, after in (("weigh", d % 2), ("silu", 2), ("product", 3 + d % 2), ("sum", 4 + d % 2)):
        MIX_AT.setdefault((start + after, stage), []).append(d)
LAST_STEP = 2 * NST


def scatters(q, n):
    found = []
    for m in range(2 * NST):
        for t, job in tile_jobs(0, m):
            if job[0] == "o" and min(m + 1, 2 * NST - 1) == q * NST + n:
                found.append((t, int(job[1])))
    return found


def build(nc, x, W_down, b_down, W_in, conv_w, conv_b, W_x, W_dt, b_dt, A_log, D_skip, W_out, ln_g, ln_b,
          W_up, b_up, gate, W1, b1, W2, b2, out, slots_dram, f_dram, s_dram):
    with ExitStack() as ctx:
        def sb(name, shape, dt=F32):
            return ctx.enter_context(nc.sbuf_tensor(name, shape, dt))

        def ps(name):
            return ctx.enter_context(nc.psum_tensor(name, [P, 512], F32))

        def sem(name):
            return ctx.enter_context(nc.semaphore(name))

        w_down = sb("w_down", [P, KD, BD])
        w_in = sb("w_in", [P, 2 * DIN])
        w_x = sb("w_x", [P, NH, 2 * NST + DTR])
        w_dt = sb("w_dt", [64, DIN])
        w_out = sb("w_out", [P, NH, BD])
        w_up = sb("w_up", [P, D])
        w_up_g = sb("w_up_g", [P, D])
        w_gate = sb("w_gate", [P, KD, E])
        b1_c = sb("b1_c", [P, E, KH])
        b_down_c = sb("b_down_c", [P, 1])
        conv_w_c = sb("conv_w_c", [P, NH, TAPS])
        conv_b_c = sb("conv_b_c", [P, NH])
        b_dt_c = sb("b_dt_c", [P, NH])
        a_log_c = sb("a_log_c", [P, NH, NST])
        a_exp = sb("a_exp", [P, NH, NST])
        a_neg = sb("a_neg", [P, NH, NST])
        d_skip_c = sb("d_skip_c", [P, NH])
        ln_g_c = sb("ln_g_c", [P, 1])
        ln_b_c = sb("ln_b_c", [P, 1])
        ln_b_wide = sb("ln_b_wide", [P, P])
        up_const = sb("up_const", [P, D])
        ident = sb("ident", [P, P])
        before = sb("before", [P, P])
        ones = sb("ones", [P, P])
        select = sb("select", [96, 2 * NST, P], BF16)
        lower = sb("lower", [P, E, E])
        eps_c = sb("eps_c", [P, 1])

        h_all = sb("h_all", [P, NSEQ, L])
        gate_lo = sb("gate_lo", [P, TOKENS // P])
        gate_hi = sb("gate_hi", [P, TOKENS // P])
        tile_expert = sb("tile_expert", [P, NT])
        tile_table = sb("tile_table", [P, 2, NT], I32)
        list_end = sb("list_end", [P, E], I32)

        state = sb("state", [P, STATES, NH, L])
        c_wide = sb("c_wide", [P, C_COPIES, L])
        shared = sb("shared", [P, 11792])

        def part(*shape, of=shared):
            nonlocal taken
            size = 1
            for k in shape:
                size *= k
            flat = of[:, taken:taken + size]
            taken += size
            names = "abcd"[:len(shape)]
            if len(shape) == 1:
                return flat
            return flat.rearrange(f"p ({' '.join(names)}) -> p {' '.join(names)}",
                                  **{k: v for k, v in list(zip(names, shape))[1:]})

        taken = 0
        rows = [part(UNIT, ROW) for _ in range(RING)]
        pad_rows = part(ST, ROW)
        early = state[:, :, :, :].rearrange("p n h t -> p (n h t)")
        taken = 0
        xnT = [part(KD, UNIT * P, of=early) for _ in range(2)]
        above = part(UNIT, E, E, of=early)
        equal = part(UNIT, E, E, of=early)
        taken = 0
        w1 = [part(KD, HID) for _ in range(2)]
        w2 = [part(KH, D) for _ in range(2)]
        slot_rows = [part(ST, ROW) for _ in range(2)]
        slotT = part(KD, SLOTS)
        hT = part(KH, SLOTS)
        y_rows = [part(ST, D) for _ in range(2)]
        b2_wide = [part(D) for _ in range(2)]
        taken = 0
        f_rows = [part(TT, 2 * D) for _ in range(MIXED)]
        s_rows = [part(TT, D) for _ in range(MIXED - 1)]
        early = h_all[:, :, :].rearrange("p s t -> p (s t)")
        taken = 0
        s_rows.append(part(TT, D, of=early))
        x_rows = [part(TT, D, of=early) for _ in range(MIXED)]
        assert taken <= (NSEQ - 1) * L

        ln_stats = sb("ln_stats", [P, UNIT, 6])
        ln_mv = sb("ln_mv", [P, UNIT, 2])
        ln_log = sb("ln_log", [P, UNIT])
        ln_rstd = sb("ln_rstd", [P, UNIT])
        logits = sb("logits", [P, UNIT, E])
        lexp = sb("lexp", [P, UNIT, E])
        prob = sb("prob", [P, UNIT, E])
        rank = sb("rank", [P, UNIT, E])
        mask = sb("mask", [P, 2, UNIT, E])
        picked = sb("picked", [P, UNIT, E])
        weight = sb("weight", [P, UNIT, E])
        slot = sb("slot", [P, UNIT, E])
        is_hi = sb("is_hi", [P, UNIT, E])
        w_hi = sb("w_hi", [P, UNIT, E])
        w_lo = sb("w_lo", [P, UNIT, E])
        e_hi = sb("e_hi", [P, UNIT, E])
        small = sb("small", [P, 8, UNIT])
        slot_lo = sb("slot_lo", [P, RING, UNIT], U32)
        slot_hi = sb("slot_hi", [P, RING, UNIT], U32)
        next_slot = sb("next_slot", [P, E])
        iotas_i = sb("iotas_i", [P, 3 * E + 16 + NT], I32)
        iotas = sb("iotas", [P, 3 * E + 16 + NT])
        list_start = iotas[:, 0:E]
        token2 = iotas[:, E:2 * E]
        expert_no = iotas[:, 2 * E:3 * E]
        tile_marks = iotas[:, 3 * E:3 * E + 16]
        tile_no = iotas[:, 3 * E + 16:]
        tile_ends = sb("tile_ends", [P, E, UNIT])
        restart = sb("restart", [P, E, UNIT])
        counts = sb("counts", [P, E])
        tiles_in = sb("tiles_in", [P, E])
        tiles_end = sb("tiles_end", [P, E])
        over_mark = sb("over_mark", [P, E, 16])
        past = sb("past", [P, NT, E])
        tile_first = sb("tile_first", [P, NT])
        tile_row = sb("tile_row", [P, NT])

        xz = sb("xz", [P, 2, 2 * NH, L])
        xdbl = sb("xdbl", [64, L])
        bc = sb("bc", [96, 2, L], BF16)
        bc_rest = sb("bc_rest", [32, L])
        bc_mid = sb("bc_mid", [32, L], BF16)
        dt_v = sb("dt_v", [P, NH, L])
        dt_m = sb("dt_m", [P, NH, L])
        dt = sb("dt", [P, 2, NH, L])
        u_sb = sb("u_sb", [P, 2, NH, L])

        decay = sb("decay", [P, 2, NH, L])

        skip = dt_m

        b1_pick = sb("b1_pick", [P, KH, E])
        b1_tile = sb("b1_tile", [P, 2, KH])
        expert_is = sb("expert_is", [P, E])
        is_high = sb("is_high", [P, ST])
        credit = sb("credit", [1, 2, ST])
        y_index = sb("y_index", [P, 2, ST], U32)

        m_sb = dt_m[:, 0, :].rearrange("p (c m) -> p c m", c=TT)
        m_stats = sb("m_stats", [P, TT, 6])
        m_mv = sb("m_mv", [P, TT, 2])
        m_log = sb("m_log", [P, TT])
        m_rstd = sb("m_rstd", [P, TT])
        mnT = dt_m[:, 1, :]
        s_out = sb("s_out", [P, TT, D])

        pB = [ps("pB0"), ps("pB1")]
        pC = ps("pC")
        pY = [ps("pY0"), ps("pY1")]
        pF = [ps("pF0"), ps("pF1")]
        pM = ps("pM")

        w_first_ready = sem("w_first_ready")
        w_ready = sem("w_ready")
        select_ready = sem("select_ready")
        b1_ready = sem("b1_ready")
        x_loaded0 = sem("x_loaded0")
        x_loaded1 = sem("x_loaded1")
        x_loaded2 = sem("x_loaded2")
        x_loaded3 = sem("x_loaded3")
        dve_consts = sem("dve_consts")
        pool_memset = sem("pool_memset")
        consts_ready = sem("consts_ready")
        iotas_ready = sem("iotas_ready")
        iotas_float = sem("iotas_float")
        conv_step = sem("conv_step")
        conv_ready = sem("conv_ready")
        w_made = sem("w_made")
        lnb_wide = sem("lnb_wide")
        lnb_up = sem("lnb_up")
        a_exp_ready = sem("a_exp_ready")
        a_ready = sem("a_ready")
        r_stats = sem("r_stats")
        r_rstd = sem("r_rstd")
        r_xn = sem("r_xn")
        r_turned = sem("r_turned")
        r_turn_read = sem("r_turn_read")
        r_logits = sem("r_logits")
        r_h = sem("r_h")
        r_h_read = sem("r_h_read")
        r_step = sem("r_step")
        r_step2 = sem("r_step2")
        r_exp = sem("r_exp")
        r_mask = sem("r_mask")
        r_place = sem("r_place")
        r_place_read = sem("r_place_read")
        r_slots = sem("r_slots")
        r_scattered0 = sem("r_scattered0")
        r_scattered1 = sem("r_scattered1")
        r_scattered2 = sem("r_scattered2")
        r_scattered3 = sem("r_scattered3")
        pads_made = sem("pads_made")
        pads_stored = sem("pads_stored")
        table_step = sem("table_step")
        table_ready = sem("table_ready")
        front_filled = sem("front_filled")
        front_drained = sem("front_drained")
        back_filled = sem("back_filled")
        back_drained = sem("back_drained")
        silu_done = sem("silu_done")
        split_step = sem("split_step")
        bc_shifted = sem("bc_shifted")
        negabs_ready = sem("negabs_ready")
        dt_exp = sem("dt_exp")
        dt_ln = sem("dt_ln")
        onep_ready = sem("onep_ready")
        dt_rest = sem("dt_rest")
        dt_ready = sem("dt_ready")
        u_ready = sem("u_ready")
        b_wide_ready = sem("b_wide_ready")
        c_wide_ready = sem("c_wide_ready")
        c_copied = sem("c_copied")
        decay_ready = sem("decay_ready")
        drive_ready = sem("drive_ready")
        rows_loaded0 = sem("rows_loaded0")
        rows_loaded1 = sem("rows_loaded1")
        bc_mid_ready = sem("bc_mid_ready")
        scanned = sem("scanned")
        seen_ready = sem("seen_ready")
        paired = sem("paired")
        foured = sem("foured")
        summed = sem("summed")
        y_read = sem("y_read")
        gated = sem("gated")
        m_stats_step = sem("m_stats_step")
        m_rstd_step = sem("m_rstd_step")
        mn_ready = sem("mn_ready")
        s_ready = sem("s_ready")
        s_stored = sem("s_stored")
        tile_loaded0 = sem("tile_loaded0")
        tile_loaded1 = sem("tile_loaded1")
        ffn_filled = sem("ffn_filled")
        ffn_free0 = sem("ffn_free0")
        ffn_free1 = sem("ffn_free1")
        b1_step = sem("b1_step")
        b1_tile_ready = sem("b1_tile_ready")
        index_step = sem("index_step")
        index_ready = sem("index_ready")
        y_ready = sem("y_ready")
        y_scattered0 = sem("y_scattered0")
        y_scattered1 = sem("y_scattered1")
        mf_loaded0 = sem("mf_loaded0")
        mf_loaded1 = sem("mf_loaded1")
        mf_loaded2 = sem("mf_loaded2")
        mf_loaded3 = sem("mf_loaded3")
        msx_loaded0 = sem("msx_loaded0")
        msx_loaded1 = sem("msx_loaded1")
        msx_loaded2 = sem("msx_loaded2")
        msx_loaded3 = sem("msx_loaded3")
        m_stored0 = sem("m_stored0")
        m_stored1 = sem("m_stored1")
        m_stored2 = sem("m_stored2")
        m_stored3 = sem("m_stored3")
        m_weighted = sem("m_weighted")
        m_added = sem("m_added")
        m_silu = sem("m_silu")
        m_mixed = sem("m_mixed")
        m_out = sem("m_out")
        sp_passed = sem("sp_passed")
        dve_passed = sem("dve_passed")
        pool_passed = sem("pool_passed")
        act_passed = sem("act_passed")
        x_loaded = [x_loaded0, x_loaded1, x_loaded2, x_loaded3]
        r_scattered = [r_scattered0, r_scattered1, r_scattered2, r_scattered3]
        rows_loaded = [rows_loaded0, rows_loaded1]
        tile_loaded = [tile_loaded0, tile_loaded1]
        ffn_free = [ffn_free0, ffn_free1]
        y_scattered = [y_scattered0, y_scattered1]
        mf_loaded = [mf_loaded0, mf_loaded1, mf_loaded2, mf_loaded3]
        msx_loaded = [msx_loaded0, msx_loaded1, msx_loaded2, msx_loaded3]
        m_stored = [m_stored0, m_stored1, m_stored2, m_stored3]

        def front_count(f, job):
            return f * len(FRONT) + FRONT.index(job) + 1

        def back_count(b, job):
            return b * len(BACK) + BACK.index(job) + 1

        def tile_pos(i, job):
            return 2 + i * len(TILE_JOBS) + TILE_JOBS.index(job) + 1

        def tile_of(k, q, t):
            return 6 * k + 3 * q + t, (q + t) % 2, 3 * k + (3 * q + t) // 2

        def later(s, n, back=4):
            return n >= back or not isinstance(s, int) or s > 0

        x_units = x.rearrange("s l d -> (s l) d").rearrange("(u c p) d -> u p c d", p=P, c=UNIT)
        x_seqs = x.rearrange("s (c p) d -> s p c d", p=P)
        out_seqs = out.rearrange("s (c p) d -> s p c d", p=P)
        s_seqs = s_dram.rearrange("(s c p) d -> s p c d", p=P, c=TT)
        f_seqs = f_dram.rearrange("(s c p two) d -> s p c (two d)", p=P, c=TT, two=2)

        def column(v, n):
            return v.rearrange("(c p) -> p c", p=P) if n > 1 else v.rearrange("(p c) -> p c", c=1)

        small_loads = [
            (w_down[:, :, :], W_down.rearrange("(k p) m -> p k m", p=P)),
            (w_gate[:, :, :], gate.rearrange("(k p) m -> p k m", p=P)),
            (b_down_c[:, :], column(b_down, 1)),
            (w_in[:, :], W_in),
            (conv_w_c[:, :, :], conv_w.rearrange("(c p) k -> p c k", p=P)),
            (w_x[:, :, 0:2 * NST], W_x.rearrange("(k p) m -> p k m", p=P)[:, :, DTR:]),
            (w_x[:, :, 2 * NST:], W_x.rearrange("(k p) m -> p k m", p=P)[:, :, 0:DTR]),
            (w_dt[32:64, :], W_dt),
            (w_out[:, :, :], W_out.rearrange("(k p) m -> p k m", p=P)),
            (w_up[:, :], W_up),
            (conv_b_c[:, :], column(conv_b, NH)),
            (b_dt_c[:, :], column(b_dt, NH)),
            (a_log_c[:, :, :], A_log.rearrange("(c p) n -> p c n", p=P)),
            (d_skip_c[:, :], column(D_skip, NH)),
            (ln_g_c[:, :], column(ln_g, 1)),
            (ln_b_c[:, :], column(ln_b, 1)),
            (up_const[:, :], b_up.partition_broadcast(P)),
        ]
        n_first = 3
        n_small = 16 * (len(small_loads) - n_first)
        n_consts = 4

        block = ctx.enter_context(nc.Block())

        @block.sync
        def _(sp):
            def load_unit(u):
                if u >= RING:
                    sp.wait_ge(r_scattered[u % RING], 16 * 2 * UNIT * (u // RING))
                sp.dma_start(rows[u % RING][:, :, 0:D], x_units[u]).then_inc(x_loaded[u % RING], 16)

            def tile_place(i):
                row = sp.value_load(tile_table[0:1, 0, bass.ds(i, 1)], min_val=0, max_val=E * REGION)
                return row, sp.value_load(tile_table[0:1, 1, bass.ds(i, 1)], min_val=0, max_val=E - 1)

            def load_rows(row, buf):
                sp.dma_start(slot_rows[buf], slots_dram[bass.ds(row, SLOTS), :].rearrange(
                    "(c p) w -> p c w", p=P)).then_inc(rows_loaded[buf], 16)

            def load_first(e, buf):
                sp.dma_start(w1[buf], W1[bass.ds(e, 1)].rearrange("o (k p) h -> p (o k) h", p=P)).then_inc(
                    tile_loaded[buf], 16)

            def load_second(e, buf):
                sp.dma_start(w2[buf], W2[bass.ds(e, 1)].rearrange("o (k p) d -> p (o k) d", p=P)).then_inc(
                    tile_loaded[buf], 16)
                sp.dma_start(b2_wide[buf], b2[bass.ds(e, 1)].rearrange("o d -> (o d)").partition_broadcast(P)).then_inc(
                    tile_loaded[buf], 16)

            def next_tile(i, buf, rows_only=False):
                sp.wait_ge(index_ready, i - 1)
                sp.wait_ge(ffn_free[1], 4 * i - 5)
                sp.sem_inc(sp_passed, 1)
                row, e = tile_place(i)
                load_rows(row, buf)
                if rows_only:
                    return
                load_first(e, buf)
                sp.wait_ge(y_ready, i - 1)
                sp.sem_inc(sp_passed, 1)
                load_second(e, buf)

            def store_s(b):
                sp.wait_ge(s_ready, b + 1)
                sp.dma_start(s_seqs[b], s_out[:, :, :]).then_inc(s_stored, 16)

            def load_mix(d):
                sp.dma_start(f_rows[d % MIXED], f_seqs[d]).then_inc(mf_loaded[d % MIXED], 16)
                if d < NSEQ - 1:
                    sp.wait_ge(s_stored, 16 * (d + 2))
                    sp.dma_start(s_rows[d % MIXED], s_seqs[d]).then_inc(msx_loaded[d % MIXED], 16)

            def load_x(d):
                if d >= MIXED:
                    sp.wait_ge(m_stored[d % MIXED], 16 * (d // MIXED))
                sp.dma_start(x_rows[d % MIXED], x_seqs[d]).then_inc(msx_loaded[d % MIXED], 16)

            def store_mix(d):
                sp.wait_ge(m_out, d + 1)
                sp.dma_start(out_seqs[d], x_rows[d % MIXED]).then_inc(m_stored[d % MIXED], 16)

            load_unit(0)
            with nc.allow_non_contiguous_dma(reason="columns of biases, once"):
                for dst, src in small_loads[:n_first]:
                    sp.dma_start(dst, src).then_inc(w_first_ready, 16)
                for u in range(1, RING):
                    load_unit(u)
                for dst, src in small_loads[n_first:]:
                    sp.dma_start(dst, src).then_inc(w_ready, 16)
                sp.dma_start(b1_c[:, :, :], b1.rearrange("e (c p) -> p e c", p=P)).then_inc(b1_ready, 16)
            for u in range(RING, NU):
                load_unit(u)
            sp.wait_ge(pads_made, 2)
            sp.wait_ge(table_ready, 1)
            for e in range(E + 1):
                row = sp.value_load(list_end[0:1, e:e + 1], min_val=0, max_val=E * REGION) if e < E else E * REGION
                sp.dma_start(slots_dram[bass.ds(row, SLOTS), :].rearrange("(c p) w -> p c w", p=P),
                             pad_rows).then_inc(pads_stored, 16)
            sp.wait_ge(pads_stored, 16 * (E + 1))
            for j in range(RING):
                sp.wait_ge(r_scattered[j], 16 * 2 * UNIT * (NU // RING))
            for i in range(2):
                row, e = tile_place(i)
                load_rows(row, i)
                load_first(e, i)
                load_second(e, i)
            sp.sem_inc(s_stored, 16)
            with sp.Fori(0, TILE_PAIRS) as k:
                for q in range(2):
                    for t in range(3):
                        i, buf, _ = tile_of(k, q, t)
                        next_tile(i + 2, buf)
                    store_s(2 * k + q)
            next_tile(TILES - 1, (TILES - 1) % 2)
            next_tile(TILES, TILES % 2, rows_only=True)
            store_s(2 * TILE_PAIRS)
            for buf in range(2):
                sp.wait_ge(y_scattered[buf], 16 * ST * ((TILES + 1 - buf) // 2 + 1))
            sp.wait_ge(front_filled, front_count(NSEQ - 2, "Z1"))
            for d in range(MIXED):
                load_mix(d)
                load_x(d)
            for d in range(0, NSEQ, 2):
                for b in (NSEQ - 3, NSEQ - 2):
                    if 4 + 4 * (d // 2) == (b - NSEQ + 3) * NST + 8:
                        store_s(b)
                for e in (d, d + 1):
                    store_mix(e)
                    if e + MIXED < NSEQ:
                        load_mix(e + MIXED)
                for e in (d + MIXED, d + 1 + MIXED):
                    if e < NSEQ:
                        load_x(e)
            for buf in range(MIXED):
                sp.wait_ge(m_stored[buf], 16 * NSEQ // MIXED)

        @block.tensor
        def _(pe):
            mm = nc.tensor.matmul
            turn_banks = [pB[0], pB[1], pC, pY[0]]

            def turn_unit(u, j):
                pe.wait_ge(r_xn, u + 1)
                for k in range(KD):
                    for half in range(2):
                        bank = turn_banks[2 * k + half]
                        for c in range(4):
                            last = nc.tensor.transpose(bank[:, c * P:(c + 1) * P],
                                                       rows[j][:, 4 * half + c, k * P:(k + 1) * P], ident[:, :])
                        last.then_inc(r_turned, 1)

            def project_unit(u, j):
                pe.wait_ge(r_turn_read, 4 * u + 4)
                for c in range(UNIT):
                    for k in range(KD):
                        last = mm(pY[1][:, c * E:(c + 1) * E], xnT[j % 2][:, k, c * P:(c + 1) * P], w_gate[:, k, :],
                                  start=(k == 0), stop=(k == KD - 1))
                last.then_inc(r_logits, 1)
                if not isinstance(u, int) or u > 0:
                    pe.wait_ge(r_h_read, 2 * u)
                for half in range(2):
                    for k in range(KD):
                        last = mm(pF[half][:, :], w_down[:, k, :], xnT[j % 2][:, k, half * L:(half + 1) * L],
                                  start=(k == 0), stop=(k == KD - 1))
                    last.then_inc(r_h, 1)

            def place_unit(u, j):
                pe.wait_ge(r_mask, u + 1)
                picks = mask[:, j % 2, :, :]
                mm(pM[:, 0:UNIT * E], before[:, :], picks.rearrange("p c e -> p (c e)"), start=True, stop=True)
                mm(pM[:, UNIT * E:2 * UNIT * E], ones[:, :], picks.rearrange("p c e -> p e c"),
                   start=True, stop=True).then_inc(r_place, 1)

            def spread(s, q, n):
                g = s * NST + n
                if n == 0:
                    pe.wait_ge(split_step, 2 * (s + 1))
                    pe.wait_ge(bc_shifted, 2 * (s + 1))
                if later(s, n, 2):
                    pe.wait_ge(drive_ready, g - 1)
                mm(pB[n % 2][:, :], select[:, n, :], bc[:, q, :], start=True, stop=True).then_inc(b_wide_ready, 1)
                if later(s, n, 1):
                    pe.wait_ge(c_copied, g)
                mm(pC[:, :], select[:, NST + n, :], bc[:, q, :], start=True, stop=True).then_inc(c_wide_ready, 1)

            def add_up(s, group):
                size = together(s)
                if size == 4:
                    pe.wait_ge(foured, s * (NST // 4) + group + 1)
                else:
                    pe.wait_ge(seen_ready, s * NST + group + 1)
                if group == 0 and later(s, 0):
                    pe.wait_ge(y_read, s)
                for half in range(NH):
                    last = mm(pY[half][:, :], ident[:, :], state[:, (group * size + size - 1) % STATES, half, :],
                              start=(group == 0), stop=(group == NST // size - 1), skip_group_check=True)
                last.then_inc(summed, 1)

            def front_job(f, q, job, back_done):
                if job != FRONT[0] or later(f, 0):
                    pe.wait_ge(front_drained, front_count(f, job) - 1)
                if back_done is not None:
                    pe.wait_ge(back_drained, back_done)
                i = int(job[1]) if len(job) > 1 else 0
                if job[0] == "V":
                    last = mm(pM[:, :], w_in[:, i * P:(i + 1) * P], h_all[:, f, :], start=True, stop=True)
                elif job[0] == "Z":
                    last = mm(pM[:, :], w_in[:, DIN + i * P:DIN + (i + 1) * P], h_all[:, f, :],
                              start=True, stop=True)
                elif job == "X":
                    pe.wait_ge(silu_done, f + 1)
                    for k in range(NH):
                        last = mm(pM[0:64, :], w_x[:, k, :], xz[:, q, k, :], start=(k == 0), stop=(k == NH - 1))
                else:
                    last = mm(pM[:, :], w_dt[32:64, i * P:(i + 1) * P], xdbl[32:64, :], start=True, stop=True)
                last.then_inc(front_filled, 1)

            def back_job(b, job, front_done):
                pe.wait_ge(front_drained, front_done)
                if job != BACK[0]:
                    pe.wait_ge(back_drained, back_count(b, job) - 1)
                if job == "M":
                    pe.wait_ge(gated, b + 1)
                    for c in range(TT):
                        for k in range(NH):
                            last = mm(pM[:, c * BD:(c + 1) * BD], skip[:, k, c * P:(c + 1) * P], w_out[:, k, :],
                                      start=(k == 0), stop=(k == NH - 1))
                elif job == "MT":
                    pe.wait_ge(mn_ready, b + 1)
                    for c in range(TT):
                        last = nc.tensor.transpose(pM[:, c * P:(c + 1) * P], m_sb[:, c, :], ident[:, :])
                else:
                    for c in range(2):
                        t = 2 * int(job[1]) + c
                        last = mm(pM[:, c * D:(c + 1) * D], mnT[:, t * P:(t + 1) * P], w_up_g[:, :],
                                  start=True, stop=True)
                last.then_inc(back_filled, 1)

            def turn_slots(buf):
                for k in range(KD):
                    for c in range(ST):
                        yield k, pF[k][:, c * P:(c + 1) * P], slot_rows[buf][:, c, k * P:(k + 1) * P]

            def expert_job(k, q, t, job):
                i, buf, done = tile_of(k, q, t)
                at = TILE_JOBS.index(job)
                bank, part_no = pF[at % 2], int(job[1])
                pe.wait_ge(ffn_free[at % 2], 1 + 4 * i + at // 2)
                if job == "h0":
                    pe.wait_ge(ffn_free[1], 1 + 4 * i)
                if job == "o0":
                    pe.wait_ge(ffn_free[1], 1 + 4 * i + 2)
                if job[0] == "h":
                    if job == "h0":
                        pe.wait_ge(tile_loaded[buf], 48 * (done + 1))
                    for kk in range(KD):
                        last = mm(bank[:, :], w1[buf][:, kk, part_no * P:(part_no + 1) * P], slotT[:, kk, :],
                                  start=(kk == 0), stop=(kk == KD - 1))
                elif job[0] == "T":
                    pe.wait_ge(rows_loaded[1 - buf], 16 * (done + 1 + buf))
                    for kk, dst, src in turn_slots(1 - buf):
                        if kk == part_no:
                            last = nc.tensor.transpose(dst, src, ident[:, :])
                else:
                    for c in range(2):
                        row_tile = 2 * part_no + c
                        for kk in range(KH):
                            last = mm(bank[:, c * D:(c + 1) * D], hT[:, kk, row_tile * P:(row_tile + 1) * P],
                                      w2[buf][:, kk, :], start=(kk == 0), stop=(kk == KH - 1))
                last.then_inc(ffn_filled, 1)

            def sequence(s, q, k=None, first=False, last=False):
                f_done, b_done = (s + 1) * len(FRONT), None

                def shared_bank_job(n, when):
                    nonlocal f_done, b_done
                    job = JOB_AT.get((n, when))
                    if job in FRONT and not last:
                        front_job(s + 1, 1 - q, job, b_done)
                        f_done = front_count(s + 1, job)
                    if job in BACK and not first:
                        back_job(s - 1, job, f_done)
                        b_done = back_count(s - 1, job)

                for n in range(NST):
                    spread(s, q, n)
                    for b, group in groups_at(s, n, SUM_LAG):
                        add_up(b, group)
                    shared_bank_job(n, 0)
                    for t, job in tile_jobs(1 - q, n) if k is not None else []:
                        expert_job(k, 1 - q, t % 3, job)
                    shared_bank_job(n, 1)

            pe.wait_ge(consts_ready, 1)
            turn_unit(0, 0)
            pe.wait_ge(dve_consts, 3)
            pe.wait_ge(lnb_wide, 1)
            pe.wait_ge(w_ready, n_small)
            mm(pM[:, 0:D], ln_b_wide[:, :], w_up[:, :], start=True, stop=True).then_inc(lnb_up, 1)
            pe.wait_ge(w_first_ready, 16 * n_first)
            pe.wait_ge(w_made, 2)
            project_unit(0, 0)
            pe.wait_ge(consts_ready, n_consts)

            def route_lap(lap, last=False):
                for j in range(RING):
                    u = lap * RING + j
                    place_unit(u, j)
                    if not last or j < RING - 1:
                        turn_unit(u + 1, (j + 1) % RING)
                        project_unit(u + 1, (j + 1) % RING)

            with pe.Fori(0, NU // RING - 1) as lap:
                route_lap(lap)
            route_lap(NU // RING - 1, last=True)
            pe.wait_ge(r_place_read, NU)
            pe.wait_ge(r_h_read, 2 * NU)
            pe.wait_ge(select_ready, 4)

            for job in FRONT:
                front_job(0, 0, job, None)
            sequence(0, 0, first=True)
            pe.wait_ge(rows_loaded[0], 16)
            for k, dst, src in turn_slots(0):
                ins = nc.tensor.transpose(dst, src, ident[:, :])
                if dst is not None and k == 0:
                    last0 = ins
            last0.then_inc(ffn_filled, 1)
            ins.then_inc(ffn_filled, 1)
            with pe.Fori(0, TILE_PAIRS) as k:
                sequence(2 * k + 1, 1, k)
                sequence(2 * k + 2, 0, k)
            sequence(NSEQ - 3, 1, TILE_PAIRS)
            sequence(NSEQ - 2, 0)
            sequence(NSEQ - 1, 1, last=True)
            for n in range(LAST_SUM + 1):
                for b, group in groups_at(NSEQ, n, SUM_LAG):
                    if b < NSEQ:
                        add_up(b, group)
            for job in BACK:
                back_job(NSEQ - 1, job, NSEQ * len(FRONT))

        @block.scalar
        def _(act):
            act_fn, copy = nc.scalar.activation, nc.scalar.copy

            def rstd(count, step, stats, mv, log, dst):
                act.wait_ge(stats, 2 * count)
                act_fn(log, mv[:, :, 1], ACT.Ln, bias=eps_c[:, :]).then_inc(step, 1)
                act.wait_ge(step, 2 * count - 1)
                act_fn(dst, log, ACT.Exp, scale=-0.5).then_inc(step, 1)

            def unit_rstd(u):
                rstd(u + 1, r_rstd, r_stats, ln_mv, ln_log[:, :], ln_rstd[:, :])

            def drain_turned(u, j):
                for k in range(KD):
                    for half in range(2):
                        act.wait_ge(r_turned, 4 * u + 2 * k + half + 1)
                        copy(xnT[j % 2][:, k, half * L:(half + 1) * L], [pB[0], pB[1], pC, pY[0]][2 * k + half][:, :]
                             ).then_inc(r_turn_read, 1)

            def drain_bottleneck(u):
                for half in range(2):
                    act.wait_ge(r_h, 2 * u + half + 1)
                    act.sem_inc(act_passed, 1)
                    act_fn(h_all[:, 2 * u + half, :], pF[half][:, :], ACT.Identity,
                           bias=b_down_c[:, :]).then_inc(r_h_read, 1)

            def unit_exp(u):
                act.wait_ge(r_step, 12 * u + 3)
                act_fn(lexp[:, :, :], lexp[:, :, :], ACT.Exp).then_inc(r_exp, 1)

            def c_copy(s, n):
                g = s * NST + n
                act.wait_ge(c_wide_ready, g + 1)
                if later(s, n, C_COPIES):
                    act.wait_ge(seen_ready, g - C_COPIES + 1)
                copy(c_wide[:, n % C_COPIES, :], pC[:, :]).then_inc(c_copied, 1)

            def decays(s, q, n):
                g = s * NST + n
                if n == 0:
                    act.wait_ge(dt_ready, s + 1)
                if later(s, n, 2):
                    act.wait_ge(scanned, g - 1)
                for half in range(NH):
                    last = act_fn(decay[:, n % 2, half, 1:], dt[:, q, half, 1:], ACT.Exp,
                                  scale=a_neg[:, half, n:n + 1])
                last.then_inc(decay_ready, 1)

            def drain_slots(i, job):
                part_no = int(job[1])
                act.wait_ge(ffn_filled, tile_pos(i - 1, job) if not isinstance(i, int) or i > 0 else part_no + 1)
                copy(slotT[:, part_no, :], pF[part_no][:, :]).then_inc(ffn_free[part_no], 1)

            def expert_drain(k, q, t, job):
                i, buf, done = tile_of(k, q, t)
                part_no = int(job[1])
                if job[0] == "h":
                    at = TILE_JOBS.index(job)
                    act.wait_ge(ffn_filled, tile_pos(i, job))
                    if job == "h0":
                        act.wait_ge(b1_tile_ready, i + 1)
                    act_fn(hT[:, part_no, :], pF[at % 2][:, :], ACT.Relu,
                           bias=b1_tile[:, buf, part_no:part_no + 1]).then_inc(ffn_free[at % 2], 1)
                elif job[0] == "T":
                    drain_slots(i + 1, job)

            def front_drain(f, q, job):
                act.wait_ge(front_filled, front_count(f, job))
                i = int(job[1]) if len(job) > 1 else 0
                if job[0] == "V":
                    if job == "V0" and later(f, 0):
                        act.wait_ge(dt_ready, f)
                        act.sem_inc(act_passed, 1)
                    ins = copy(dt_v[:, i, :], pM[:, :])
                elif job[0] == "Z":
                    if job == "Z0" and (not isinstance(f, int) or f > 1):
                        act.wait_ge(gated, f - 1)
                    ins = copy(xz[:, q, NH + i, :], pM[:, :])
                elif job == "X":
                    copy(xdbl[:, :], pM[0:64, :])
                    if later(f, 0):
                        act.wait_ge(b_wide_ready, f * NST - NST)
                        act.sem_inc(act_passed, 1)
                    ins = copy(bc[0:32, q, :], pM[0:32, :])
                else:
                    ins = act_fn(dt_v[:, i, :], pM[:, :], ACT.Identity, bias=b_dt_c[:, i:i + 1])
                ins.then_inc(front_drained, 1)

            def silu_front(f, q):
                act.wait_ge(front_drained, front_count(f, "Z1"))
                act.wait_ge(conv_ready, f + 1)
                act_fn(xz[:, q, :, :], xz[:, q, :, :], ACT.Silu).then_inc(silu_done, 1)

            def middle_part(f):
                act.wait_ge(split_step, 2 * f + 1)
                copy(bc_mid[:, :], bc_rest[:, :]).then_inc(bc_mid_ready, 1)

            def shift_parts(f, q):
                act.wait_ge(split_step, 2 * f + 2)
                copy(bc[32:64, q, :], bc_mid[:, :]).then_inc(bc_shifted, 1)
                copy(bc[64:96, q, :], bc_rest[:, :]).then_inc(bc_shifted, 1)

            def dt_exps(f, q):
                act.wait_ge(negabs_ready, f + 1)
                act_fn(u_sb[:, q, :, :], dt_m[:, :, :], ACT.Exp).then_inc(dt_exp, 1)
                act.wait_ge(dt_exp, f + 1)
                act_fn(dt[:, q, :, :], u_sb[:, q, :, :], ACT.Ln, bias=1.0).then_inc(dt_ln, 1)

            def back_copy(b, job):
                act.wait_ge(back_filled, back_count(b, job))
                src = pM[:, :].rearrange("p (c m) -> p c m", c=TT) if job == "M" else pM[:, :]
                copy(m_sb if job == "M" else mnT, src).then_inc(back_drained, 1)

            def front_step(f, q, n, when):
                if JOB_AT.get((n, when)) in FRONT:
                    front_drain(f, q, JOB_AT[n, when])
                if (n, when) == (7, 0):
                    silu_front(f, q)
                if (n, when) == (10, 1):
                    middle_part(f)
                if (n, when) == (12, 0):
                    shift_parts(f, q)
                    dt_exps(f, q)

            def back_step(b, n, when):
                if JOB_AT.get((n, when)) in ("M", "MT"):
                    back_copy(b, JOB_AT[n, when])
                if (n, when) == (8, 0):
                    rstd(b + 1, m_rstd_step, m_stats_step, m_mv, m_log[:, :], m_rstd[:, :])

            def sequence(s, q, k=None, first=False, last=False):
                for n in range(NST):
                    c_copy(s, n)
                    if n < NST - 1:
                        decays(s, q, n + 1)
                    for when in range(2):
                        if not last:
                            front_step(s + 1, 1 - q, n, when)
                        if not first:
                            back_step(s - 1, n, when)
                        for t, job in tile_jobs(1 - q, n) if k is not None and when == 0 else []:
                            expert_drain(k, 1 - q, t % 3, job)
                    if n == NST - 1 and not last:
                        decays(s + 1, 1 - q, 0)
                    if isinstance(s, int) and s >= NSEQ - 2:
                        mix_step((s - NSEQ + 2) * NST + n)

            def mix_step(step):
                for d in MIX_AT.get((step, "silu"), []):
                    act.wait_ge(m_added, d + 1)
                    both = f_rows[d % MIXED]
                    act_fn(both[:, :, 0:D], both[:, :, 0:D], ACT.Silu).then_inc(m_silu, 1)

            act.wait_ge(dve_consts, 3)
            unit_rstd(0)
            drain_turned(0, 0)
            act.wait_ge(w_first_ready, 16 * n_first)
            act.wait_ge(w_ready, n_small)
            act_fn(a_exp[:, :, :], a_log_c[:, :, :], ACT.Exp).then_inc(a_exp_ready, 1)
            act.wait_ge(a_exp_ready, 1)
            nc.scalar.mul(a_neg[:, :, :], a_exp[:, :, :], -1.0).then_inc(a_ready, 1)
            act.wait_ge(a_ready, 1)

            def route_lap(lap, last=False):
                for j in range(RING):
                    u = lap * RING + j
                    unit_exp(u)
                    there_is_next = not last or j < RING - 1
                    if there_is_next:
                        unit_rstd(u + 1)
                    drain_bottleneck(u)
                    if there_is_next:
                        drain_turned(u + 1, (j + 1) % RING)

            with act.Fori(0, NU // RING - 1) as lap:
                route_lap(lap)
            route_lap(NU // RING - 1, last=True)
            for job in FRONT:
                front_drain(0, 0, job)
                if job == "Z1":
                    silu_front(0, 0)
            middle_part(0)
            shift_parts(0, 0)
            dt_exps(0, 0)
            decays(0, 0, 0)
            sequence(0, 0, first=True)
            for job in ("T0", "T1"):
                drain_slots(0, job)
            with act.Fori(0, TILE_PAIRS) as k:
                sequence(2 * k + 1, 1, k)
                sequence(2 * k + 2, 0, k)
            sequence(NSEQ - 3, 1, TILE_PAIRS)
            sequence(NSEQ - 2, 0)
            sequence(NSEQ - 1, 1, last=True)
            for step in range(LAST_STEP, LAST_STEP + 3):
                mix_step(step)
            for n in range(NST):
                for when in range(2):
                    back_step(NSEQ - 1, n, when)

        @block.vector
        def _(dve):
            tt, ts, stt = nc.vector.tensor_tensor, nc.vector.tensor_scalar, nc.vector.scalar_tensor_tensor
            reduce, vcopy = nc.vector.tensor_reduce, nc.vector.tensor_copy

            def statistics(count, step, n, src, stats, mv):
                for c in range(n):
                    last = nc.vector.bn_stats(stats[:, c, :], src(c))
                last.then_inc(step, 1)
                dve.wait_ge(step, 2 * count - 1)
                dve.sem_inc(dve_passed, 1)
                for c in range(n):
                    last = nc.vector.bn_aggr(mv[:, c, :], stats[:, c, :])
                last.then_inc(step, 1)
                dve.wait_ge(step, 2 * count)

            def measure_unit(u, j, laps):
                dve.wait_ge(x_loaded[j], 16 * (laps + 1))
                statistics(u + 1, r_stats, UNIT, lambda c: rows[j][:, c, 0:D], ln_stats, ln_mv)

            def normalise_unit(u, j):
                dve.wait_ge(r_rstd, 2 * (u + 1))
                for c in range(UNIT):
                    last = ts(rows[j][:, c, 0:D], rows[j][:, c, 0:D], ln_mv[:, c, 0:1], ln_rstd[:, c:c + 1],
                              ALU.subtract, ALU.mult)
                last.then_inc(r_xn, 1)

            def wide(v):
                return v.unsqueeze(2).broadcast_to([P, UNIT, E])

            lmax, lsum, linv, psum_k, guarded, pinv, hi, both = (small[:, i, :] for i in range(8))

            def choose_unit(u, j):
                count = 12 * u

                def step(ins):
                    nonlocal count
                    ins.then_inc(r_step, 1)
                    count = count + 1
                    dve.wait_ge(r_step, count)

                dve.wait_ge(r_logits, u + 1)
                step(vcopy(logits[:, :, :], pY[1][:, 0:UNIT * E].rearrange("p (c e) -> p c e", c=UNIT)))
                step(reduce(lmax, logits[:, :, :], AX.X, ALU.max))
                step(tt(lexp[:, :, :], logits[:, :, :], wide(lmax), ALU.subtract))
                dve.wait_ge(r_exp, u + 1)
                step(reduce(lsum, lexp[:, :, :], AX.X, ALU.add))
                step(nc.vector.reciprocal(linv, lsum))
                step(tt(prob[:, :, :], lexp[:, :, :], wide(linv), ALU.mult))
                rivals = prob[:, :, :].unsqueeze(2).broadcast_to([P, UNIT, E, E])
                own = prob[:, :, :].unsqueeze(3).broadcast_to([P, UNIT, E, E])
                tt(above, rivals, own, ALU.is_gt)
                step(tt(equal, rivals, own, ALU.is_equal))
                low = lower[:, :, :].rearrange("p i j -> p (i j)").unsqueeze(1).broadcast_to([P, UNIT, E * E])
                flat = "p c i j -> p c (i j)"
                step(tt(equal.rearrange(flat), equal.rearrange(flat), low, ALU.mult))
                step(tt(above, above, equal, ALU.add))
                step(reduce(rank[:, :, :], above, AX.X, ALU.add))
                ts(mask[:, j % 2, :, :], rank[:, :, :], float(TOP_K), None, ALU.is_lt).then_inc(r_mask, 1)
                dve.wait_ge(r_mask, u + 1)
                step(tt(picked[:, :, :], mask[:, j % 2, :, :], prob[:, :, :], ALU.mult))
                step(reduce(psum_k, picked[:, :, :], AX.X, ALU.add))

            def weigh_unit(u, j):
                count = 15 * u

                def step2(ins):
                    nonlocal count
                    ins.then_inc(r_step2, 1)
                    count = count + 1
                    dve.wait_ge(r_step2, count)

                step2(ts(guarded, psum_k, 1e-12, None, ALU.max))
                step2(nc.vector.reciprocal(pinv, guarded))
                tt(weight[:, :, :], picked[:, :, :], wide(pinv), ALU.mult)
                dve.wait_ge(r_place, u + 1)
                of_tile = pM[:, UNIT * E:2 * UNIT * E]
                step2(nc.vector.tensor_tensor_scan(tile_ends[:, :, :].rearrange("p e c -> p (e c)"),
                                                   restart[:, :, :].rearrange("p e c -> p (e c)"),
                                                   of_tile, 0.0, ALU.mult, ALU.add))
                step2(tt(tile_ends[:, :, :], tile_ends[:, :, :],
                         next_slot[:, :].unsqueeze(2).broadcast_to([P, E, UNIT]), ALU.add))
                vcopy(next_slot[:, :], tile_ends[:, :, UNIT - 1])
                step2(tt(slot[:, :, :], pM[:, 0:UNIT * E].rearrange("p (c e) -> p c e", c=UNIT),
                         tile_ends[:, :, :].rearrange("p e c -> p c e"), ALU.add))
                tt(slot[:, :, :], slot[:, :, :], of_tile.rearrange("p (e c) -> p c e", c=UNIT),
                   ALU.subtract).then_inc(r_place_read, 1)
                dve.wait_ge(r_place_read, u + 1)
                step2(tt(slot[:, :, :], slot[:, :, :], mask[:, j % 2, :, :], ALU.mult))
                reduce(both, slot[:, :, :], AX.X, ALU.add)
                step2(reduce(hi, slot[:, :, :], AX.X, ALU.max))
                tt(slot_lo[:, j, :], both, hi, ALU.subtract)
                vcopy(slot_hi[:, j, :], hi)
                step2(tt(is_hi[:, :, :], slot[:, :, :], wide(hi), ALU.is_equal))
                tt(e_hi[:, :, :], is_hi[:, :, :], expert_no.unsqueeze(1).broadcast_to([P, UNIT, E]), ALU.mult)
                step2(tt(w_hi[:, :, :], is_hi[:, :, :], weight[:, :, :], ALU.mult))
                step2(tt(w_lo[:, :, :], weight[:, :, :], w_hi[:, :, :], ALU.subtract))
                step2(vcopy(rows[j][:, :, D], token2))
                step2(ts(token2, token2, float(2 * UNIT * P), None, ALU.add))
                step2(reduce(rows[j][:, :, D + 1], e_hi[:, :, :], AX.X, ALU.add))
                step2(reduce(gate_hi[:, bass.ds(u * UNIT, UNIT)], w_hi[:, :, :], AX.X, ALU.add))
                step2(reduce(gate_lo[:, bass.ds(u * UNIT, UNIT)], w_lo[:, :, :], AX.X, ALU.add))
                dve.sem_inc(r_slots, 1)

            def make_table():
                count = 0

                def step(ins):
                    nonlocal count
                    ins.then_inc(table_step, 1)
                    count += 1
                    dve.wait_ge(table_step, count)

                def tiles_by(v):
                    return v.unsqueeze(1).broadcast_to([P, NT, E])

                step(tt(counts[:, :], next_slot[:, :], list_start, ALU.subtract))
                step(tt(over_mark[:, :, :], counts[:, :].unsqueeze(2).broadcast_to([P, E, 16]),
                        tile_marks.unsqueeze(1).broadcast_to([P, E, 16]), ALU.is_gt))
                step(reduce(tiles_in[:, :], over_mark[:, :, :], AX.X, ALU.add))
                step(nc.vector.tensor_tensor_scan(tiles_end[:, :], ones[:, 0:E], tiles_in[:, :], 0.0,
                                                  ALU.mult, ALU.add))
                step(tt(past[:, :, :], tile_no.unsqueeze(2).broadcast_to([P, NT, E]), tiles_by(tiles_end[:, :]),
                        ALU.is_ge))
                step(reduce(tile_expert[:, :], past[:, :, :], AX.X, ALU.add))
                step(tt(past[:, :, :], past[:, :, :], tiles_by(tiles_end[:, :]), ALU.mult))
                step(reduce(tile_first[:, :], past[:, :, :], AX.X, ALU.max))
                step(tt(tile_row[:, :], tile_no, tile_first[:, :], ALU.subtract))
                step(ts(tile_row[:, :], tile_row[:, :], float(SLOTS), None, ALU.mult))
                step(stt(tile_row[:, :], tile_expert[:, :], float(REGION), tile_row[:, :], ALU.mult, ALU.add))
                step(ts(tile_table[:, 0, :], tile_row[:, :], float(E * REGION), None, ALU.min))
                step(ts(tile_expert[:, :], tile_expert[:, :], float(E - 1), None, ALU.min))
                step(vcopy(tile_table[:, 1, :], tile_expert[:, :]))
                step(vcopy(list_end[:, :], next_slot[:, :]))
                dve.sem_inc(table_ready, 1)

            def add_pair(s, group, pair):
                a = 4 * group % STATES + 2 * pair
                dve.wait_ge(seen_ready, s * NST + 4 * group + 2 * pair + 2)
                tt(state[:, a + 1, :, :], state[:, a, :, :], state[:, a + 1, :, :], ALU.add).then_inc(paired, 1)

            def add_four(s, group):
                a = 4 * group % STATES
                dve.wait_ge(paired, s * PAIRS + 2 * group + 2)
                tt(state[:, a + 3, :, :], state[:, a + 1, :, :], state[:, a + 3, :, :], ALU.add).then_inc(foured, 1)

            def add_states_at(s, n):
                for pair in range(2):
                    for b, group in groups_at(s, n, PAIR_LAG[pair]):
                        add_pair(b, group, pair)
                for b, group in groups_at(s, n, FOUR_LAG):
                    add_four(b, group)

            def scan(s, q, n):
                g = s * NST + n
                dve.wait_ge(b_wide_ready, g + 1)
                if n == 0:
                    dve.wait_ge(u_ready, s + 1)
                if later(s, n, STATES):
                    b, m = (s, n - STATES) if n >= STATES else (s - 1, n - STATES + NST)
                    if together(b) == 1:
                        dve.wait_ge(summed, sums_before(b) + m + 1)
                    elif m % 4 == 3:
                        dve.wait_ge(summed, sums_before(b) + m // 4 + 1)
                    elif m % 4 == 1:
                        dve.wait_ge(foured, b * (NST // 4) + m // 4 + 1)
                    else:
                        dve.wait_ge(paired, b * PAIRS + m // 2 + 1)
                tt(state[:, n % STATES, :, :], u_sb[:, q, :, :],
                   pB[n % 2][:, :].unsqueeze(1).broadcast_to([P, NH, L]), ALU.mult).then_inc(drive_ready, 1)
                dve.wait_ge(drive_ready, g + 1)
                dve.wait_ge(decay_ready, g + 1)
                place = state[:, n % STATES, :, :].rearrange("p h t -> p (h t)")
                nc.vector.tensor_tensor_scan(place, decay[:, n % 2, :, :].rearrange("p h t -> p (h t)"), place,
                                             0.0, ALU.mult, ALU.add).then_inc(scanned, 1)

            def pick_bias(i, buf):
                dve.wait_ge(b1_ready, 16)
                ts(expert_is[:, :], expert_no, tile_expert[:, bass.ds(i, 1)], None, ALU.is_equal).then_inc(b1_step, 1)
                dve.wait_ge(b1_step, 2 * i + 1)
                tt(b1_pick[:, :, :], b1_c[:, :, :].rearrange("p e c -> p c e"),
                   expert_is[:, :].unsqueeze(1).broadcast_to([P, KH, E]), ALU.mult).then_inc(b1_step, 1)
                dve.wait_ge(b1_step, 2 * i + 2)
                reduce(b1_tile[:, buf, :], b1_pick[:, :, :], AX.X, ALU.add).then_inc(b1_tile_ready, 1)

            def expert_drain(k, q, t, job):
                i, buf, done = tile_of(k, q, t)
                if job == "T0":
                    dve.wait_ge(y_scattered[buf], 16 * ST * (done + 1))
                    dve.wait_ge(rows_loaded[buf], 16 * (done + 1))
                    ts(is_high[:, :], slot_rows[buf][:, :, D + 1], tile_expert[:, bass.ds(i, 1)], None,
                       ALU.is_equal).then_inc(index_step, 1)
                    dve.wait_ge(index_step, i + 1)
                    tt(y_index[:, buf, :], slot_rows[buf][:, :, D], is_high[:, :], ALU.add).then_inc(index_ready, 1)
                    pick_bias(i + 1, 1 - buf)
                if job[0] != "o":
                    return
                at, part_no = TILE_JOBS.index(job), int(job[1])
                if job == "o0":
                    dve.wait_ge(tile_loaded[buf], 48 * (done + 1))
                dve.wait_ge(ffn_filled, tile_pos(i, job))
                tt(y_rows[buf][:, 2 * part_no:2 * part_no + 2, :], pF[at % 2][:, :].rearrange("p (c d) -> p c d", c=2),
                   b2_wide[buf].unsqueeze(1).broadcast_to([P, 2, D]), ALU.add).then_inc(ffn_free[at % 2], 1)
                if job == "o1":
                    dve.wait_ge(ffn_free[1], 1 + 4 * i + at // 2 + 1)
                    dve.wait_ge(ffn_free[0], 1 + 4 * i + at // 2 + 1)
                    dve.sem_inc(y_ready, 1)

            def convolve(f, q):
                dve.wait_ge(front_drained, front_count(f, "V1"))
                if not isinstance(f, int) or f > 1:
                    dve.wait_ge(gated, f - 1)
                for i in range(NH):
                    last = ts(xz[:, q, i, :], dt_v[:, i, :], conv_w_c[:, i, TAPS - 1:TAPS], conv_b_c[:, i:i + 1],
                              ALU.mult, ALU.add)
                for back in range(1, TAPS):
                    last.then_inc(conv_step, 1)
                    dve.wait_ge(conv_step, (TAPS - 1) * f + back)
                    tap = TAPS - 1 - back
                    for i in range(NH):
                        last = stt(xz[:, q, i, back:], dt_v[:, i, :L - back], conv_w_c[:, i, tap:tap + 1],
                                   xz[:, q, i, back:], ALU.mult, ALU.add)
                last.then_inc(conv_ready, 1)

            def front_step(f, q, n, when):
                if (n, when) == (6, 0):
                    convolve(f, q)
                if (n, when) == (11, 1):
                    dve.wait_ge(front_drained, front_count(f, "D1"))
                    if later(f, 0):
                        dve.wait_ge(u_ready, f)
                    stt(dt_m[:, :, :], dt_v[:, :, :], -1.0, dt_v[:, :, :], ALU.mult, ALU.min).then_inc(
                        negabs_ready, 1)
                if (n, when) == (12, 1):
                    dve.wait_ge(dt_exp, f + 1)
                    ts(dt_m[:, :, :], u_sb[:, q, :, :], 1.0, 1.0, ALU.add, ALU.subtract).then_inc(onep_ready, 1)
                if (n, when) == (14, 0):
                    dve.wait_ge(dt_rest, 2 * (f + 1))
                    stt(dt[:, q, :, :], dt_v[:, :, :], 0.0, dt_m[:, :, :], ALU.max, ALU.add).then_inc(dt_ready, 1)

            def skip_term(b, qb):
                dve.wait_ge(summed, sums_before(b + 1))
                for half in range(NH):
                    last = stt(skip[:, half, :], xz[:, qb, half, :], d_skip_c[:, half:half + 1],
                               pY[half][:, :], ALU.mult, ALU.add)
                last.then_inc(y_read, 1)

            def back_step(b, n, when):
                if (n, when) == (8, 0):
                    dve.wait_ge(back_drained, back_count(b, "M"))
                    statistics(b + 1, m_stats_step, TT, lambda c: m_sb[:, c, :], m_stats, m_mv)
                if (n, when) == (9, 0):
                    dve.wait_ge(m_rstd_step, 2 * (b + 1))
                    for c in range(TT):
                        last = ts(m_sb[:, c, :], m_sb[:, c, :], m_mv[:, c, 0:1], m_rstd[:, c:c + 1],
                                  ALU.subtract, ALU.mult)
                    last.then_inc(mn_ready, 1)
                job = JOB_AT.get((n, when))
                if job in ("S0", "S1"):
                    j = int(job[1])
                    if j == 0:
                        dve.wait_ge(s_stored, 16 * (b + 1))
                    dve.wait_ge(back_filled, back_count(b, job))
                    tt(s_out[:, 2 * j:2 * j + 2, :], pM[:, :].rearrange("p (c d) -> p c d", c=2),
                       up_const[:, :].unsqueeze(1).broadcast_to([P, 2, D]), ALU.add).then_inc(back_drained, 1)
                    if j == 1:
                        dve.wait_ge(back_drained, back_count(b, "S1"))
                        dve.sem_inc(s_ready, 1)

            def sequence(s, q, k=None, first=False, last=False):
                for n in range(NST):
                    add_states_at(s, n)
                    scan(s, q, n)
                    if n == LAST_SUM and not first:
                        skip_term(s - 1, 1 - q)
                    for when in range(2):
                        if not last:
                            front_step(s + 1, 1 - q, n, when)
                        if not first:
                            back_step(s - 1, n, when)
                        for t, job in tile_jobs(1 - q, n) if k is not None and when == 0 else []:
                            expert_drain(k, 1 - q, t % 3, job)
                    if isinstance(s, int) and s >= NSEQ - 2:
                        mix_step((s - NSEQ + 2) * NST + n)

            def mix_step(step):
                for d in MIX_AT.get((step, "weigh"), []):
                    both = f_rows[d % MIXED]
                    dve.wait_ge(mf_loaded[d % MIXED], 16 * (d // MIXED + 1))
                    for c in range(TT):
                        last = ts(both[:, c, 0:D], both[:, c, 0:D], gate_lo[:, d * TT + c:d * TT + c + 1], None,
                                  ALU.mult)
                    last.then_inc(m_weighted, 1)
                    dve.wait_ge(m_weighted, d + 1)
                    for c in range(TT):
                        last = stt(both[:, c, 0:D], both[:, c, D:], gate_hi[:, d * TT + c:d * TT + c + 1],
                                   both[:, c, 0:D], ALU.mult, ALU.add)
                    last.then_inc(m_added, 1)
                for d in MIX_AT.get((step, "sum"), []):
                    dve.wait_ge(m_mixed, d + 1)
                    tt(x_rows[d % MIXED], s_rows[d % MIXED], x_rows[d % MIXED], ALU.add).then_inc(m_out, 1)

            nc.vector.memset(ones[:, :], 1.0).then_inc(dve_consts, 1)
            nc.vector.memset(eps_c[:, :], EPS).then_inc(dve_consts, 1)
            nc.vector.memset(decay[:, :, :, 0:1], 0.0).then_inc(dve_consts, 1)
            dve.wait_ge(dve_consts, 3)
            measure_unit(0, 0, 0)
            normalise_unit(0, 0)
            dve.wait_ge(consts_ready, n_consts)
            dve.wait_ge(w_ready, n_small)
            ts(ln_b_wide[:, :], ones[:, :], ln_b_c[:, :], None, ALU.mult).then_inc(lnb_wide, 1)
            dve.wait_ge(lnb_up, 1)
            tt(up_const[:, :], up_const[:, :], pM[:, 0:D], ALU.add).then_inc(w_made, 1)
            ts(w_up_g[:, :], w_up[:, :], ln_g_c[:, :], None, ALU.mult).then_inc(w_made, 1)
            dve.wait_ge(w_made, 2)
            vcopy(iotas[:, :], iotas_i[:, :]).then_inc(iotas_float, 1)
            dve.wait_ge(iotas_float, 1)
            vcopy(next_slot[:, :], list_start).then_inc(iotas_float, 1)
            nc.vector.memset(restart[:, :, :], 1.0).then_inc(iotas_float, 1)
            dve.wait_ge(iotas_float, 3)
            nc.vector.memset(restart[:, :, 0:1], 0.0).then_inc(iotas_float, 1)
            dve.wait_ge(iotas_float, 4)

            def route_lap(lap, last=False):
                for j in range(RING):
                    u = lap * RING + j
                    there_is_next = not last or j < RING - 1
                    if there_is_next:
                        measure_unit(u + 1, (j + 1) % RING, lap + (j + 1) // RING)
                    choose_unit(u, j)
                    if there_is_next:
                        normalise_unit(u + 1, (j + 1) % RING)
                    weigh_unit(u, j)

            with dve.Fori(0, NU // RING - 1) as lap:
                route_lap(lap)
            route_lap(NU // RING - 1, last=True)
            nc.vector.memset(pad_rows, 0.0).then_inc(pads_made, 1)
            dve.wait_ge(pads_made, 1)
            nc.vector.memset(pad_rows[:, :, D], NO_TOKEN).then_inc(pads_made, 1)
            make_table()

            convolve(0, 0)
            dve.wait_ge(front_drained, front_count(0, "X"))
            tt(bc_rest[:, :], xdbl[0:32, :], bc[0:32, 0, :], ALU.subtract).then_inc(split_step, 1)
            dve.wait_ge(bc_mid_ready, 1)
            tt(bc_rest[:, :], bc_rest[:, :], bc_mid[:, :], ALU.subtract).then_inc(split_step, 1)
            front_step(0, 0, 11, 1)
            front_step(0, 0, 12, 1)
            dve.wait_ge(onep_ready, 1)
            tt(dt_m[:, :, :], u_sb[:, 0, :, :], dt_m[:, :, :], ALU.subtract).then_inc(dt_rest, 1)
            dve.wait_ge(dt_rest, 1)
            dve.wait_ge(dt_ln, 1)
            tt(dt_m[:, :, :], dt_m[:, :, :], dt[:, 0, :, :], ALU.add).then_inc(dt_rest, 1)
            front_step(0, 0, 14, 0)
            dve.wait_ge(dt_ready, 1)
            dve.wait_ge(silu_done, 1)
            tt(u_sb[:, 0, :, :], dt[:, 0, :, :], xz[:, 0, 0:NH, :], ALU.mult).then_inc(u_ready, 1)
            sequence(0, 0, first=True)
            pick_bias(0, 0)
            with dve.Fori(0, TILE_PAIRS) as k:
                sequence(2 * k + 1, 1, k)
                sequence(2 * k + 2, 0, k)
            sequence(NSEQ - 3, 1, TILE_PAIRS)
            sequence(NSEQ - 2, 0)
            sequence(NSEQ - 1, 1, last=True)
            skip_term(NSEQ - 1, 1)
            for step in range(LAST_STEP, LAST_STEP + 4):
                mix_step(step)
            for n in range(NST):
                for when in range(2):
                    back_step(NSEQ - 1, n, when)
            mix_step(LAST_STEP + 4)
            mix_step(LAST_STEP + 5)

        @block.gpsimd
        def _(pool):
            tt, copy = nc.gpsimd.tensor_tensor, nc.gpsimd.tensor_copy

            def scatter_unit(u, j):
                pool.wait_ge(r_slots, u + 1)
                pool.sem_inc(pool_passed, 1)
                for c in range(UNIT):
                    for index in (slot_lo, slot_hi):
                        nc.gpsimd.indirect_dma_start(
                            slots_dram, bass.IndirectOffsetOnAxis(ap=index[:, j, c:c + 1], axis=0),
                            rows[j][:, c, :], None).then_inc(r_scattered[j], 16)

            def scatter_tile(k, q, t, half):
                i, buf, done = tile_of(k, q, t)
                pool.wait_ge(index_ready, i + 1)
                pool.wait_ge(ffn_free[half], 1 + 4 * i + 4)
                pool.sem_inc(pool_passed, 1)
                for c in range(2 * half, 2 * half + 2):
                    nc.gpsimd.indirect_dma_start(
                        f_dram, bass.IndirectOffsetOnAxis(ap=y_index[:, buf, c:c + 1], axis=0),
                        y_rows[buf][:, c, :], None, bounds_check=2 * TOKENS - 1,
                        oob_is_err=False).then_inc(y_scattered[buf], 16)

            def see(s, n):
                g = s * NST + n
                pool.wait_ge(scanned, g + 1)
                pool.wait_ge(c_copied, g + 1)
                tt(state[:, n % STATES, :, :], state[:, n % STATES, :, :],
                   c_wide[:, n % C_COPIES, :].unsqueeze(1).broadcast_to([P, NH, L]), ALU.mult).then_inc(seen_ready, 1)

            def front_step(f, q, n):
                if n == 9:
                    pool.wait_ge(front_drained, front_count(f, "X"))
                    tt(bc_rest[:, :], xdbl[0:32, :], bc[0:32, q, :], ALU.subtract).then_inc(split_step, 1)
                if n == 11:
                    pool.wait_ge(bc_mid_ready, f + 1)
                    tt(bc_rest[:, :], bc_rest[:, :], bc_mid[:, :], ALU.subtract).then_inc(split_step, 1)
                if n == 13:
                    pool.wait_ge(onep_ready, f + 1)
                    tt(dt_m[:, :, :], u_sb[:, q, :, :], dt_m[:, :, :], ALU.subtract).then_inc(dt_rest, 1)
                    pool.wait_ge(dt_rest, 2 * f + 1)
                    pool.wait_ge(dt_ln, f + 1)
                    tt(dt_m[:, :, :], dt_m[:, :, :], dt[:, q, :, :], ALU.add).then_inc(dt_rest, 1)
                if n == 14:
                    pool.wait_ge(dt_ready, f + 1)
                    pool.wait_ge(silu_done, f + 1)
                    tt(u_sb[:, q, :, :], dt[:, q, :, :], xz[:, q, 0:NH, :], ALU.mult).then_inc(u_ready, 1)

            def gate_y(b, qb):
                pool.wait_ge(y_read, b + 1)
                tt(skip[:, :, :], skip[:, :, :], xz[:, qb, NH:, :], ALU.mult).then_inc(gated, 1)

            def mix_step(step):
                for d in MIX_AT.get((step, "product"), []):
                    pool.wait_ge(m_silu, d + 1)
                    rounds = d // MIXED
                    block_out = s_rows[d % MIXED] if d < NSEQ - 1 else s_out[:, :, :]
                    pool.wait_ge(msx_loaded[d % MIXED], 32 * rounds + (32 if d < NSEQ - 1 else 16))
                    if d == NSEQ - 1:
                        pool.wait_ge(s_ready, NSEQ)
                    tt(s_rows[d % MIXED], block_out, f_rows[d % MIXED][:, :, 0:D], ALU.mult).then_inc(m_mixed, 1)

            def sequence(s, q, k=None, first=False, last=False, tiles_before=0):
                for n in range(NST):
                    see(s, n)
                    if n == LAST_SUM and not first:
                        gate_y(s - 1, 1 - q)
                    if not last:
                        front_step(s + 1, 1 - q, n)
                    for t, half in scatters(1 - q, n):
                        if k is not None or t < tiles_before:
                            scatter_tile(TILE_PAIRS if k is None else k, t // 3, t % 3, half)
                    if isinstance(s, int) and s >= NSEQ - 2:
                        mix_step((s - NSEQ + 2) * NST + n)

            nc.gpsimd.memset(ident[:, :], 0.0).then_inc(pool_memset, 1)
            nc.gpsimd.memset(before[:, :], 1.0).then_inc(pool_memset, 1)
            nc.gpsimd.memset(lower[:, :, :], 1.0).then_inc(pool_memset, 1)
            pool.wait_ge(pool_memset, 3)
            nc.gpsimd.affine_select(out=ident[:, :], in_=ident[:, :], compare_op=ALU.not_equal, fill=1.0, base=0,
                                    pattern=[[-1, P]], channel_multiplier=1).then_inc(consts_ready, 1)
            nc.gpsimd.affine_select(out=before[:, :], in_=before[:, :], compare_op=ALU.is_gt, fill=0.0, base=0,
                                    pattern=[[1, P]], channel_multiplier=-1).then_inc(consts_ready, 1)
            nc.gpsimd.affine_select(out=lower[:, :, :], in_=lower[:, :, :], compare_op=ALU.is_gt, fill=0.0, base=0,
                                    pattern=[[1, E], [-1, E]], channel_multiplier=0).then_inc(consts_ready, 1)
            at = 0
            for width, step, per_partition in ((E, REGION, 0), (E, 2 * P, 2), (E, 1, 0), (16, SLOTS, 0), (NT, 1, 0)):
                ins = nc.gpsimd.iota(iotas_i[:, at:at + width], pattern=[[step, width]], base=0,
                                     channel_multiplier=per_partition)
                ins.then_inc(iotas_ready, 1)
                at += width
            pool.wait_ge(consts_ready, 3)
            pool.wait_ge(iotas_ready, 5)
            pool.sem_inc(consts_ready, 1)
            nc.gpsimd.memset(select[:, :, :], 0.0).then_inc(select_ready, 1)
            for part_no in range(3):
                pool.wait_ge(select_ready, 1 + part_no)
                nc.gpsimd.affine_select(out=select[:, :, :], in_=select[:, :, :], compare_op=ALU.not_equal, fill=1.0,
                                        base=-32 * part_no, pattern=[[-1, 2 * NST], [0, P]],
                                        channel_multiplier=1).then_inc(select_ready, 1)

            pool.wait_ge(dve_consts, 2)
            for buf in range(2):
                for c in range(ST):
                    pool.dma_start(credit[0:1, buf, c:c + 1], eps_c[0:1, :]).then_inc(y_scattered[buf], 16)

            with pool.Fori(0, NU // RING) as lap:
                for j in range(RING):
                    scatter_unit(lap * RING + j, j)
            sequence(0, 0, first=True)
            with pool.Fori(0, TILE_PAIRS) as k:
                sequence(2 * k + 1, 1, k)
                sequence(2 * k + 2, 0, k)
            sequence(NSEQ - 3, 1, TILE_PAIRS)
            sequence(NSEQ - 2, 0, tiles_before=3)
            sequence(NSEQ - 1, 1, last=True)
            gate_y(NSEQ - 1, 1)
            mix_step(LAST_STEP)
            mix_step(LAST_STEP + 3)
            mix_step(LAST_STEP + 4)


_INS = ["L0_attn_x", "L0_attn_W_down", "L0_attn_b_down", "L0_attn_W_in", "L0_attn_conv_w", "L0_attn_conv_b",
        "L0_attn_W_x", "L0_attn_W_dt", "L0_attn_b_dt", "L0_attn_A_log", "L0_attn_D_skip", "L0_attn_W_out",
        "L0_attn_ln_g", "L0_attn_ln_b", "L0_attn_W_up", "L0_attn_b_up", "L0_ffn_gate", "L0_ffn_W1", "L0_ffn_b1",
        "L0_ffn_W2", "L0_ffn_b2"]


def kernel(**inputs):
    import numpy as _np
    import concourse.bacc as _bacc
    from concourse import mybir as _mybir
    from concourse.bass_utils import run_bass_kernel_spmd as _run

    nc = _bacc.Bacc("TRN2", target_bir_lowering=False, num_devices=1)
    arrays, args = {}, []
    for name in _INS:
        a = _np.ascontiguousarray(inputs[name])
        arrays[f"in_{name}_dram"] = a
        args.append(nc.dram_tensor(f"in_{name}_dram", a.shape, _mybir.dt.from_np(a.dtype), kind="ExternalInput").ap())
    args.append(nc.dram_tensor("out_0_dram", (NSEQ, L, D), _mybir.dt.from_np(_np.dtype("float32")),
                               kind="ExternalOutput").ap())
    f32 = _mybir.dt.from_np(_np.dtype("float32"))
    args.append(nc.dram_tensor("slots_dram", (E * REGION + SLOTS, ROW), f32).ap())
    args.append(nc.dram_tensor("f_dram", (TOP_K * TOKENS, D), f32).ap())
    args.append(nc.dram_tensor("s_dram", (TOKENS, D), f32).ap())
    build(nc, *args)
    r = _run(nc, [arrays], core_ids=[0])
    return r.results[0]["out_0_dram"]
```
